# Optimizing a Trainium2 kernel written in Bass

```python
import numpy as np
import jax
import jax.numpy as jnp

def _softmax(x, axis=-1):
    return jax.nn.softmax(x, axis=axis)

def _gelu(x):
    return jax.nn.gelu(x, approximate=True)

def _silu(x):
    return jax.nn.silu(x)

def _sigmoid(x):
    return jax.nn.sigmoid(x)

def _layernorm(x, axis=-1, eps=1e-05):
    m = jnp.mean(x, axis=axis, keepdims=True)
    v = jnp.var(x, axis=axis, keepdims=True)
    return (x - m) / jnp.sqrt(v + eps)

def _scatter_add(tgt, idx, src, axis=0):
    return tgt.at[idx].add(src)

def _segment_sum(src, seg, n):
    return jax.ops.segment_sum(src, seg, n)
kernel_name = 'mk_xattn_ffn_d2_seqx_r8_8129e5'

def setup_inputs(seed: int=0):
    np.random.seed(seed)
    _w = jnp.asarray

    def _rec_inputs():
        import jax
        import jax.numpy as jnp
        _rk = jax.random.key(seed)
        x = 0.0002417 + 0.9998 * jax.random.normal(jax.random.fold_in(_rk, 1), (4, 256, 128), jnp.float32)
        _lenS = 256 - jax.random.randint(jax.random.fold_in(_rk, 7), (4,), 0, max(1, 256 // 4) + 1, jnp.int32)
        _lenS2 = 512 - jax.random.randint(jax.random.fold_in(_rk, 8), (4,), 0, max(1, 512 // 4) + 1, jnp.int32)
        _ctx_1024P = jax.random.normal(jax.random.fold_in(_rk, 11), (4, 16, 128), jnp.float32)
        _ctx_1024c = jax.random.dirichlet(jax.random.fold_in(_rk, 511), 0.3 * jnp.ones((16,), jnp.float32), (4, 512))
        _ctx_1024t = jnp.einsum('bsk,bkd->bsd', _ctx_1024c, _ctx_1024P)
        _ctx_1024t = _ctx_1024t * jax.lax.rsqrt(jnp.mean(jnp.square(_ctx_1024t)) + 1e-12) * 0.953939
        ctx_1024 = 7.22013e-05 + 1.00017 * (_ctx_1024t + 0.3 * jax.random.normal(jax.random.fold_in(_rk, 611), (4, 512, 128), jnp.float32))
        _validS = jnp.arange(256)[None, :] < _lenS[:, None]
        _validS2 = jnp.arange(512)[None, :] < _lenS2[:, None]
        _causal = jnp.tril(jnp.ones((256, 256), dtype=bool))
        mask_1x1xSxS2_ik0 = jnp.where(jnp.broadcast_to(_validS2[0:1, None, None, :], (1, 1, 256, 512)), 0, 1).astype(jnp.int32)
        return (x, ctx_1024, mask_1x1xSxS2_ik0)
    x, ctx_1024, mask_1x1xSxS2_ik0 = _rec_inputs()

    def _L0_xattn_setup():
        import jax, jax.numpy as jnp
        import numpy as np
        EMBED = 128
        HEADS = 16
        HEAD_DIM = EMBED // HEADS
        key = jax.random.key(seed)
        ks = jax.random.split(key, 8)
        B, S, D = (4, 256, EMBED)
        s = 1.0 / np.sqrt(D)
        return {'values': jax.random.normal(ks[0], (B, S, D), jnp.float32), 'keys': jax.random.normal(ks[1], (B, S, D), jnp.float32), 'query': jax.random.normal(ks[2], (B, S, D), jnp.float32), 'Wv': jax.random.normal(ks[3], (D, D), jnp.float32) * s, 'Wk': jax.random.normal(ks[4], (D, D), jnp.float32) * s, 'Wq': jax.random.normal(ks[5], (D, D), jnp.float32) * s, 'Wo': jax.random.normal(ks[6], (D, D), jnp.float32) * s, 'bo': jax.random.normal(ks[7], (D,), jnp.float32) * 0.01}
    _L0_xattn_all = _L0_xattn_setup()
    _L0_xattn_in = {k: v for k, v in _L0_xattn_all.items() if k in ('Wv', 'Wk', 'Wq', 'Wo', 'bo')}
    del _L0_xattn_all

    def _L0_ffn_setup():
        import jax, jax.numpy as jnp
        import numpy as np
        S, B, D, H, DH = (512, 8, 128, 16, 64)

        def _forward(x, Wg, Wq, bq, Wkv, bkv, Wo, bo, ln_g, ln_b):
            s_len, bsz, d_model = x.shape
            n_head, _, d_head = Wq.shape
            cap = s_len // n_head
            scale = 1.0 / d_head ** 0.5
            h = jnp.transpose(x, (1, 0, 2))
            t = h
            probs = jax.nn.softmax(h @ Wg, axis=-1)
            scores = jnp.transpose(probs, (0, 2, 1))
            _, idx = jax.lax.top_k(scores, cap)
            idx = jnp.sort(idx, axis=-1)
            hg = jnp.take_along_axis(h[:, None, :, :], idx[..., None], axis=2)
            hg = jnp.transpose(hg, (1, 0, 2, 3))
            q = jnp.einsum('hbcd,hde->hbce', hg, Wq) + bq[:, None, None, :]
            kv = jnp.einsum('hbcd,hde->hbce', hg, Wkv) + bkv[:, None, None, :]
            k, v = jnp.split(kv, 2, axis=-1)
            att = jnp.einsum('hbid,hbjd->hbij', q, k) * scale
            p = jax.nn.softmax(att, axis=1)
            av = jnp.einsum('hbij,hbjd->hbid', p, v)
            ao = jnp.einsum('hbid,hde->hbie', av, Wo) + bo
            tok = jnp.transpose(idx, (1, 0, 2))
            b_ids = jnp.arange(bsz)[None, :, None]
            outs = jnp.zeros_like(t).at[b_ids, tok].add(ao)
            y = t + outs
            mu = jnp.mean(y, axis=-1, keepdims=True)
            var = jnp.var(y, axis=-1, keepdims=True)
            yn = (y - mu) * jax.lax.rsqrt(var + 1e-05) * ln_g + ln_b
            return jnp.transpose(yn, (1, 0, 2))
        key = jax.random.key(seed)
        ks = jax.random.split(key, 6)
        s = 0.02
        return {'x': jax.random.normal(ks[0], (S, B, D), jnp.float32), 'attn_mask': jnp.zeros((S, S), jnp.bool_), 'Wg': jax.random.normal(ks[1], (D, H), jnp.float32) * s, 'Wq': jax.random.normal(ks[2], (H, D, DH), jnp.float32) * s, 'bq': jnp.zeros((H, DH), jnp.float32), 'Wkv': jax.random.normal(ks[3], (H, D, 2 * DH), jnp.float32) * s, 'bkv': jnp.zeros((H, 2 * DH), jnp.float32), 'Wo': jax.random.normal(ks[4], (H, DH, D), jnp.float32) * s, 'bo': jnp.zeros((D,), jnp.float32), 'ln_g': jnp.ones((D,), jnp.float32), 'ln_b': jnp.zeros((D,), jnp.float32)}
    _L0_ffn_all = _L0_ffn_setup()
    _L0_ffn_in = {k: v for k, v in _L0_ffn_all.items() if k in ('attn_mask', 'Wg', 'Wq', 'bq', 'Wkv', 'bkv', 'Wo', 'bo', 'ln_g', 'ln_b')}
    del _L0_ffn_all

    def _L1_xattn_setup():
        import jax, jax.numpy as jnp
        import numpy as np
        D_MODEL = 128
        HEADS = 16
        D_K = D_MODEL // HEADS
        B, S = (2, 256)
        key = jax.random.key(seed)
        ks = jax.random.split(key, 11)
        sc = 1.0 / np.sqrt(D_MODEL)
        inp = {'q': jax.random.normal(ks[0], (B, S, D_MODEL), jnp.float32), 'k': jax.random.normal(ks[1], (B, S, D_MODEL), jnp.float32), 'v': jax.random.normal(ks[2], (B, S, D_MODEL), jnp.float32), 'mask': jnp.tril(jnp.ones((S, S), jnp.int32))[None, None], 'w_q': jax.random.normal(ks[3], (D_MODEL, D_MODEL), jnp.float32) * sc, 'b_q': jax.random.normal(ks[4], (D_MODEL,), jnp.float32) * sc, 'w_k': jax.random.normal(ks[5], (D_MODEL, D_MODEL), jnp.float32) * sc, 'b_k': jax.random.normal(ks[6], (D_MODEL,), jnp.float32) * sc, 'w_v': jax.random.normal(ks[7], (D_MODEL, D_MODEL), jnp.float32) * sc, 'b_v': jax.random.normal(ks[8], (D_MODEL,), jnp.float32) * sc, 'w_o': jax.random.normal(ks[9], (D_MODEL, D_MODEL), jnp.float32) * sc, 'b_o': jax.random.normal(ks[10], (D_MODEL,), jnp.float32) * sc}
        return inp
    _L1_xattn_all = _L1_xattn_setup()
    _L1_xattn_in = {k: v for k, v in _L1_xattn_all.items() if k in ('w_q', 'b_q', 'w_k', 'b_k', 'w_v', 'b_v', 'w_o', 'b_o')}
    del _L1_xattn_all

    def _L1_ffn_setup():
        import jax, jax.numpy as jnp
        import numpy as np
        B, S, D_MODEL, D_HIDDEN = (4, 256, 128, 512)

        def act_quant(x):
            scale = 127.0 / jnp.clip(jnp.max(jnp.abs(x), axis=-1, keepdims=True), 1e-05)
            return jnp.clip(jnp.round(x * scale), -128, 127) / scale

        def weight_quant(w):
            scale = 1.0 / jnp.clip(jnp.mean(jnp.abs(w)), 1e-05)
            return jnp.clip(jnp.round(w * scale), -1, 1) / scale

        def bit_linear(x, w):
            xq = x + jax.lax.stop_gradient(act_quant(x) - x)
            wq = w + jax.lax.stop_gradient(weight_quant(w) - w)
            return jnp.einsum('bsd,hd->bsh', xq, wq)

        def depthwise_conv1d(x_bcl, w, b):
            y = jax.lax.conv_general_dilated(x_bcl, w, window_strides=(1,), padding=[(1, 1)], dimension_numbers=('NCH', 'OIH', 'NCH'), feature_group_count=x_bcl.shape[1])
            return y + b[None, :, None]
        key = jax.random.key(seed)
        ks = jax.random.split(key, 5)
        lim1 = 1.0 / np.sqrt(D_MODEL)
        lim2 = 1.0 / np.sqrt(D_HIDDEN)
        limc = 1.0 / np.sqrt(3.0)
        return {'x': jax.random.normal(ks[0], (B, S, D_MODEL), dtype=jnp.float32), 'w1': jax.random.uniform(ks[1], (D_HIDDEN, D_MODEL), jnp.float32, -lim1, lim1), 'conv_w': jax.random.uniform(ks[2], (D_HIDDEN, 1, 3), jnp.float32, -limc, limc), 'conv_b': jax.random.uniform(ks[3], (D_HIDDEN,), jnp.float32, -limc, limc), 'w2': jax.random.uniform(ks[4], (D_MODEL, D_HIDDEN), jnp.float32, -lim2, lim2)}
    _L1_ffn_all = _L1_ffn_setup()
    _L1_ffn_in = {k: v for k, v in _L1_ffn_all.items() if k in ('w1', 'conv_w', 'conv_b', 'w2')}
    del _L1_ffn_all
    return {'x': x, 'ctx_1024': ctx_1024, 'mask_1x1xSxS2_ik0': mask_1x1xSxS2_ik0, 'L0_xattn_Wv': _L0_xattn_in['Wv'], 'L0_xattn_Wk': _L0_xattn_in['Wk'], 'L0_xattn_Wq': _L0_xattn_in['Wq'], 'L0_xattn_Wo': _L0_xattn_in['Wo'], 'L0_xattn_bo': _L0_xattn_in['bo'], 'L0_ffn_attn_mask': _L0_ffn_in['attn_mask'], 'L0_ffn_Wg': _L0_ffn_in['Wg'], 'L0_ffn_Wq': _L0_ffn_in['Wq'], 'L0_ffn_bq': _L0_ffn_in['bq'], 'L0_ffn_Wkv': _L0_ffn_in['Wkv'], 'L0_ffn_bkv': _L0_ffn_in['bkv'], 'L0_ffn_Wo': _L0_ffn_in['Wo'], 'L0_ffn_bo': _L0_ffn_in['bo'], 'L0_ffn_ln_g': _L0_ffn_in['ln_g'], 'L0_ffn_ln_b': _L0_ffn_in['ln_b'], 'L1_xattn_w_q': _L1_xattn_in['w_q'], 'L1_xattn_b_q': _L1_xattn_in['b_q'], 'L1_xattn_w_k': _L1_xattn_in['w_k'], 'L1_xattn_b_k': _L1_xattn_in['b_k'], 'L1_xattn_w_v': _L1_xattn_in['w_v'], 'L1_xattn_b_v': _L1_xattn_in['b_v'], 'L1_xattn_w_o': _L1_xattn_in['w_o'], 'L1_xattn_b_o': _L1_xattn_in['b_o'], 'L1_ffn_w1': _L1_ffn_in['w1'], 'L1_ffn_conv_w': _L1_ffn_in['conv_w'], 'L1_ffn_conv_b': _L1_ffn_in['conv_b'], 'L1_ffn_w2': _L1_ffn_in['w2']}

def reference(x, ctx_1024, mask_1x1xSxS2_ik0, L0_xattn_Wv, L0_xattn_Wk, L0_xattn_Wq, L0_xattn_Wo, L0_xattn_bo, L0_ffn_attn_mask, L0_ffn_Wg, L0_ffn_Wq, L0_ffn_bq, L0_ffn_Wkv, L0_ffn_bkv, L0_ffn_Wo, L0_ffn_bo, L0_ffn_ln_g, L0_ffn_ln_b, L1_xattn_w_q, L1_xattn_b_q, L1_xattn_w_k, L1_xattn_b_k, L1_xattn_w_v, L1_xattn_b_v, L1_xattn_w_o, L1_xattn_b_o, L1_ffn_w1, L1_ffn_conv_w, L1_ffn_conv_b, L1_ffn_w2):
    import jax
    import jax.numpy as jnp

    def _L0_xattn_ref(values, keys, query, Wv, Wk, Wq, Wo, bo):
        import jax, jax.numpy as jnp
        import numpy as np
        EMBED = 128
        HEADS = 16
        HEAD_DIM = EMBED // HEADS
        N, Lq, D = query.shape
        Lk = keys.shape[1]
        Lv = values.shape[1]
        v = (values @ Wv.T).reshape(N, Lv, HEADS, HEAD_DIM)
        k = (keys @ Wk.T).reshape(N, Lk, HEADS, HEAD_DIM)
        q = (query @ Wq.T).reshape(N, Lq, HEADS, HEAD_DIM)
        energy = jnp.einsum('nqhd,nkhd->nhqk', q, k)
        attn = jax.nn.softmax(energy / jnp.sqrt(jnp.float32(D)), axis=3)
        out = jnp.einsum('nhql,nlhd->nqhd', attn, v).reshape(N, Lq, D)
        return out @ Wo.T + bo

    def _L0_ffn_ref(x, attn_mask, Wg, Wq, bq, Wkv, bkv, Wo, bo, ln_g, ln_b):
        import jax, jax.numpy as jnp
        import numpy as np
        S, B, D, H, DH = (512, 8, 128, 16, 64)

        def _forward(x, Wg, Wq, bq, Wkv, bkv, Wo, bo, ln_g, ln_b):
            s_len, bsz, d_model = x.shape
            n_head, _, d_head = Wq.shape
            cap = s_len // n_head
            scale = 1.0 / d_head ** 0.5
            h = jnp.transpose(x, (1, 0, 2))
            t = h
            probs = jax.nn.softmax(h @ Wg, axis=-1)
            scores = jnp.transpose(probs, (0, 2, 1))
            _, idx = jax.lax.top_k(scores, cap)
            idx = jnp.sort(idx, axis=-1)
            hg = jnp.take_along_axis(h[:, None, :, :], idx[..., None], axis=2)
            hg = jnp.transpose(hg, (1, 0, 2, 3))
            q = jnp.einsum('hbcd,hde->hbce', hg, Wq) + bq[:, None, None, :]
            kv = jnp.einsum('hbcd,hde->hbce', hg, Wkv) + bkv[:, None, None, :]
            k, v = jnp.split(kv, 2, axis=-1)
            att = jnp.einsum('hbid,hbjd->hbij', q, k) * scale
            p = jax.nn.softmax(att, axis=1)
            av = jnp.einsum('hbij,hbjd->hbid', p, v)
            ao = jnp.einsum('hbid,hde->hbie', av, Wo) + bo
            tok = jnp.transpose(idx, (1, 0, 2))
            b_ids = jnp.arange(bsz)[None, :, None]
            outs = jnp.zeros_like(t).at[b_ids, tok].add(ao)
            y = t + outs
            mu = jnp.mean(y, axis=-1, keepdims=True)
            var = jnp.var(y, axis=-1, keepdims=True)
            yn = (y - mu) * jax.lax.rsqrt(var + 1e-05) * ln_g + ln_b
            return jnp.transpose(yn, (1, 0, 2))
        return _forward(x, Wg, Wq, bq, Wkv, bkv, Wo, bo, ln_g, ln_b)

    def _L1_xattn_ref(q, k, v, mask, w_q, b_q, w_k, b_k, w_v, b_v, w_o, b_o):
        import jax, jax.numpy as jnp
        import numpy as np
        D_MODEL = 128
        HEADS = 16
        D_K = D_MODEL // HEADS
        B, S = (2, 256)
        b = q.shape[0]
        Q = q @ w_q.T + b_q
        K = k @ w_k.T + b_k
        V = v @ w_v.T + b_v
        Q = Q.reshape(b, -1, HEADS, D_K).transpose(0, 2, 1, 3)
        K = K.reshape(b, -1, HEADS, D_K).transpose(0, 2, 1, 3)
        V = V.reshape(b, -1, HEADS, D_K).transpose(0, 2, 1, 3)
        scores = jnp.einsum('bhqd,bhkd->bhqk', Q, K) / np.sqrt(D_K).astype(np.float32)
        scores = jnp.where(mask == 0, -jnp.inf, scores)
        attn = jax.nn.softmax(scores, axis=-1)
        out = jnp.einsum('bhqk,bhkd->bhqd', attn, V)
        out = out.transpose(0, 2, 1, 3).reshape(b, -1, D_MODEL)
        return out @ w_o.T + b_o

    def _L1_ffn_ref(x, w1, conv_w, conv_b, w2):
        import jax, jax.numpy as jnp
        import numpy as np
        B, S, D_MODEL, D_HIDDEN = (4, 256, 128, 512)

        def act_quant(x):
            scale = 127.0 / jnp.clip(jnp.max(jnp.abs(x), axis=-1, keepdims=True), 1e-05)
            return jnp.clip(jnp.round(x * scale), -128, 127) / scale

        def weight_quant(w):
            scale = 1.0 / jnp.clip(jnp.mean(jnp.abs(w)), 1e-05)
            return jnp.clip(jnp.round(w * scale), -1, 1) / scale

        def bit_linear(x, w):
            xq = x + jax.lax.stop_gradient(act_quant(x) - x)
            wq = w + jax.lax.stop_gradient(weight_quant(w) - w)
            return jnp.einsum('bsd,hd->bsh', xq, wq)

        def depthwise_conv1d(x_bcl, w, b):
            y = jax.lax.conv_general_dilated(x_bcl, w, window_strides=(1,), padding=[(1, 1)], dimension_numbers=('NCH', 'OIH', 'NCH'), feature_group_count=x_bcl.shape[1])
            return y + b[None, :, None]
        h = bit_linear(x, w1)
        h = depthwise_conv1d(h.transpose(0, 2, 1), conv_w, conv_b)
        h = h.transpose(0, 2, 1)
        h = jax.nn.silu(h)
        return bit_linear(h, w2)
    x = x + _L0_xattn_ref(ctx_1024, ctx_1024, _layernorm(x, axis=-1), L0_xattn_Wv, L0_xattn_Wk, L0_xattn_Wq, L0_xattn_Wo, L0_xattn_bo)
    x = x + _L0_ffn_ref(_layernorm(x, axis=-1), L0_ffn_attn_mask, L0_ffn_Wg, L0_ffn_Wq, L0_ffn_bq, L0_ffn_Wkv, L0_ffn_bkv, L0_ffn_Wo, L0_ffn_bo, L0_ffn_ln_g, L0_ffn_ln_b)
    x = x + _L1_xattn_ref(_layernorm(x, axis=-1), ctx_1024, ctx_1024, mask_1x1xSxS2_ik0, L1_xattn_w_q, L1_xattn_b_q, L1_xattn_w_k, L1_xattn_b_k, L1_xattn_w_v, L1_xattn_b_v, L1_xattn_w_o, L1_xattn_b_o)
    x = x + _L1_ffn_ref(_layernorm(x, axis=-1), L1_ffn_w1, L1_ffn_conv_w, L1_ffn_conv_b, L1_ffn_w2)
    return x

_drawn_inputs = setup_inputs


def setup_inputs(seed=0):
    import zlib

    import numpy as np

    out = dict(_drawn_inputs(seed))
    spreads = {'L0_ffn_bq': (0.0, 0.1),
     'L0_ffn_bkv': (0.0, 0.1),
     'L0_ffn_bo': (0.0, 0.1),
     'L0_ffn_ln_g': (1.0, 0.2),
     'L0_ffn_ln_b': (0.0, 0.1)}
    factors = {'L0_xattn_bo': 6.269, 'L1_xattn_b_q': 6.036, 'L1_xattn_b_k': 8.0}
    for name, (base, spread) in spreads.items():
        noise = np.random.default_rng([zlib.crc32(name.encode()), seed]).standard_normal(out[name].shape)
        drawn = base * np.exp(spread * noise) if base else spread * noise
        out[name] = jnp.asarray(drawn.astype(out[name].dtype))
    for name, factor in factors.items():
        out[name] = (out[name] * factor).astype(out[name].dtype)
    return out
```

```python
import concourse.bass as bass
from concourse import mybir
from contextlib import ExitStack

B, S, D = 4, 256, 128
SK = 512
H, DH = 16, 8
HID = 512
QT, KT, CH = S // 128, SK // 128, HID // 128
HG = 4
NJ = H // HG
EPS = 1e-5
SCALES = (D ** -0.5, DH ** -0.5)
ROUND = 12582912.0
MASK_MAX, MASK_EXP = -1e30, -3e38

BLOCKS = [(0, 0), (0, 1), (0, 2), (1, 0), (0, 3), (1, 1), (1, 2), (1, 3)]
NB = len(BLOCKS)
AT_BLOCK = {lb: k for k, lb in enumerate(BLOCKS)}
UNITS = NB * NJ
STEPS = UNITS * KT
LEAD = 3
PER_BLOCK = NJ * KT
NST = 3
NM = 3
NP = 4


def schedule():
    at = {}

    def add(step, *task):
        at.setdefault(step, []).append(task)

    for k, (layer, b) in enumerate(BLOCKS):
        s = PER_BLOCK * k - 28
        old = AT_BLOCK.get((layer, b - 2))
        free = PER_BLOCK * (old + 1) if old is not None else -99
        if layer == 0:
            add(s, "stats", k, 0)
            add(s + 1, "norm", k, 0)
            add(s + 2, "x_t", k, 0)
            add(s + 3, "proj_q", k, 0)
            add(s + 3, "split_q", k, 0)
            add(s + 4, "write_q", k, 0)
            add(s + 4, "add_bo", k, 0)
            add(max(s + 7, free), "read_q", k, 0)
        add(s + 1, "proj_k", k, 0)
        add(s + 1, "split_k", k, 0)
        add(s + 3, "write_k", k, 0)
        add(max(s + 6, free), "read_k", k, 0)
        add(max(s + 5, free + 1), "proj_v", k, 0)
        e = PER_BLOCK * (k + 1)
        add(e + 2, "out_t", k, 0)
        add(e + 3, "out_t", k, 1)
        add(e + 4, "heads_t", k, 0)
        add(e + 5, "proj_o", k, 0)
        add(e + 6, "stats", k, 1)
        add(e + 7, "norm", k, 1)
        if layer == 0:
            k1 = AT_BLOCK[(1, b)]
            old = AT_BLOCK.get((1, b - 2))
            free = PER_BLOCK * (old + 1) if old is not None else -99
            add(e + 8, "stats", k, 2)
            add(e + 9, "norm", k, 2)
            add(e + 11, "stats", k1, 0)
            add(e + 12, "norm", k1, 0)
            add(e + 13, "x_t", k1, 0)
            add(e + 14, "proj_q", k1, 0)
            add(e + 14, "split_q", k1, 0)
            add(e + 14, "add_bo", k1, 0)
            add(e + 15, "write_q", k1, 0)
            add(max(e + 17, free), "read_q", k1, 0)
        else:
            add(e + 8, "quant_x", k, 0)
            add(e + 9, "xq_t", k, 0)
            add(e + 10, "spread_scale", k, 0)
            add(e + 11, "up", k, 0)
            add(e + 12, "up", k, 1)
            add(e + 13, "conv", k, 0)
            add(e + 15, "silu", k, 0)
            add(e + 17, "hid_t", k, 0)
            add(e + 18, "hid_t", k, 1)
            add(e + 18, "quant_h", k, 0)
            add(e + 19, "quant_h", k, 1)
            add(e + 20, "hq_t", k, 0)
            add(e + 21, "hq_t", k, 1)
            add(e + 22, "down", k, 0)
            add(e + 23, "store", k, 0)
    for u in range(UNITS):
        add(KT * (u - LEAD + 1), "split_max", u, 0)
        add(KT * (u - LEAD + 1) + 2, "max_t", u, 0)
    add(3, "mask", 0, 0)
    add(5, "weight_mean", 0, 0)
    add(6, "quant_w", 0, 0)
    return at


TASKS = schedule()
FIRST, LAST = min(TASKS), max(max(TASKS), STEPS)
ORDER = [task for step in range(FIRST, LAST + 1) for task in TASKS.get(step, [])]
JOBS = ("proj_k", "x_t", "proj_q", "proj_v", "out_t", "heads_t", "proj_o", "xq_t", "spread_scale", "up",
        "hid_t", "hq_t", "down", "max_t", "weight_mean")
JOB = {task: n for n, task in enumerate(t for t in ORDER if t[0] in JOBS)}
NTH = {}
for _task in ORDER:
    NTH[_task] = sum(1 for t in NTH if t[0] == _task[0])


def build(nc, x, ctxT, projT, rows, cols, mask, maskT, w1T, conv, w2T, out):
    f32, bf16, i32 = mybir.dt.float32, mybir.dt.bfloat16, mybir.dt.int32
    ALU = mybir.AluOpType
    ACT = mybir.ActivationFunctionType
    X = mybir.AxisListType.X
    BO0, GAMMA, BETA, BO1, BV1 = range(5)

    k_scratch = nc.dram_tensor("k_scratch", [NB, 3, 128, SK], bf16).ap()
    q_scratch = nc.dram_tensor("q_scratch", [NB, 6, 128, S], bf16).ap()

    es = ExitStack()
    with es:
        def sb(name, shape, dt=f32):
            return es.enter_context(nc.sbuf_tensor(name, shape, dt))

        def sem(name):
            return es.enter_context(nc.semaphore(name))

        res = sb("res", [128, B, QT, D])
        ctx_sb = sb("ctx_sb", [128, B, SK])
        proj = sb("proj", [128, 8, D])
        rows_sb = sb("rows_sb", [128, 5, D])
        cols_sb = sb("cols_sb", [128, 2])
        mask_i = sb("mask_i", [128, QT, SK], i32)
        maskT_i = sb("maskT_i", [128, KT, S], i32)
        w1_sb = sb("w1_sb", [128, HID])
        w2_sb = sb("w2_sb", [128, CH, D])
        conv_sb = sb("conv_sb", [128, CH, 4])
        id32 = sb("id32", [128, 128])
        id16 = sb("id16", [128, 128], bf16)
        ones = sb("ones", [128, 128])
        ones16 = sb("ones16", [128, 512], bf16)
        zeros16 = sb("zeros16", [128, 256], bf16)
        neghalf = sb("neghalf", [128, QT])
        kst = [[sb(f"kst{l}{i}", [128, H // 2, SK], bf16) for i in range(2)] for l in range(2)]
        qst = [[sb(f"qst{l}{i}", [128, H, S], bf16) for i in range(2)] for l in range(2)]
        vst = [[sb(f"vst{l}{i}", [128, KT, H, 32]) for i in range(2)] for l in range(2)]
        mask_max = sb("mask_max", [128, QT, SK])
        mask_exp = sb("mask_exp", [128, KT, 2, S], bf16)
        masked = sb("masked", [128, 2, SK], bf16)
        k_f = sb("k_f", [128, SK])
        k_rest = sb("k_rest", [128, SK])
        k_parts = sb("k_parts", [128, 3, SK], bf16)
        q_f = sb("q_f", [128, S])
        q_rest = sb("q_rest", [128, S])
        q_parts = sb("q_parts", [128, 3, S], bf16)
        row_max = [sb(f"row_max{i}", [128, QT, HG]) for i in range(2)]
        neg_max = sb("neg_max", [128, QT, HG])
        max_parts = [sb(f"max_parts{i}", [128, QT, 2, HG], bf16) for i in range(2)]
        max_rows = [sb(f"max_rows{i}", [2 * HG, S], bf16) for i in range(2)]
        probs = [sb(f"probs{i}", [128, HG, S]) for i in range(NP)]
        o_raw = sb("o_raw", [128, NJ, S])
        inv_den = sb("inv_den", [128, NJ, HG])
        o_heads = sb("o_heads", [128, QT, H, DH])
        o_t = sb("o_t", [128, S])
        bn = [sb(f"bn{i}", [128, QT, 6]) for i in range(NM)]
        moments = [sb(f"moments{i}", [128, QT, 2]) for i in range(NM)]
        var_eps = [sb(f"var_eps{i}", [128, QT]) for i in range(NM)]
        rstd = [sb(f"rstd{i}", [128, QT]) for i in range(NM)]
        xq = [sb(f"xq{l}", [128, QT, D]) for l in range(2)]
        z = sb("z", [128, QT, D])
        xf = sb("xf", [128, QT, D])
        x_t = sb("x_t", [128, S])
        w_sum = sb("w_sum", [128, 2])
        w_mean = sb("w_mean", [128, 2])
        w_inv = sb("w_inv", [128, 2])
        w1_q = sb("w1_q", [128, HID], bf16)
        w2_q = sb("w2_q", [128, CH, D], bf16)
        amax = sb("amax", [128, QT])
        a_inv = sb("a_inv", [128, QT])
        a_scale = sb("a_scale", [128, QT])
        a_back = sb("a_back", [128, QT])
        a_tmp = sb("a_tmp", [128, QT, D])
        a_q = sb("a_q", [128, QT, D], bf16)
        back_diag = sb("back_diag", [128, QT, 128])
        a_t = sb("a_t", [128, S], bf16)
        back_rows = sb("back_rows", [128, S])
        hid = sb("hid", [128, CH, S + 2])
        y = sb("y", [128, CH, S])
        w_tmp = y[:, 0:2, :].rearrange("p c s -> p (c s)")
        tanh_y = sb("tanh_y", [128, CH, S])
        h_max = sb("h_max", [128, QT])
        h_inv = sb("h_inv", [128, QT])
        h_scale = sb("h_scale", [128, QT])
        h_back = sb("h_back", [128, QT])
        h_tmp = sb("h_tmp", [128, QT, HID])
        h_q = sb("h_q", [128, QT, HID], bf16)
        h_t = sb("h_t", [128, QT, CH, 128], bf16)
        y_out = sb("y_out", [128, QT, D])

        st = [es.enter_context(nc.psum_tensor(f"st{i}", [128, 2, S], f32)) for i in range(NST)]
        sm = [es.enter_context(nc.psum_tensor(f"sm{i}", [128, SK], f32)) for i in range(2)]
        pv = es.enter_context(nc.psum_tensor("pv", [128, 512], f32))
        sides = [es.enter_context(nc.psum_tensor(f"side{i}", [128, 512], f32)) for i in range(2)]
        sides16 = [a[:, :].bitcast(bf16) for a in sides]

        x_in = [sem(f"x_in{i}") for i in range(2)]
        ctx_in = [sem(f"ctx_in{i}") for i in range(2)]
        proj_in = sem("proj_in")
        small_in = sem("small_in")
        mask_in = sem("mask_in")
        ffn_in = sem("ffn_in")
        k_written, q_written = sem("k_written"), sem("q_written")
        kq_read = [sem(f"kq_read{k}") for k in range(NB)]
        max_placed = [sem(f"max_placed{i}") for i in range(2)]
        stored = sem("stored")
        id_set, ones_set, ones16_set, v_set, hid_set = (
            sem(n) for n in ("id_set", "ones_set", "ones16_set", "v_set", "hid_set"))
        k_ones = [sem(f"k_ones{i}") for i in range(4)]
        q_zeros, v1_set = sem("q_zeros"), sem("v1_set")
        sm_filled, max_taken = sem("sm_filled"), sem("max_taken")
        st_filled, exp_done, pv_done, pv_emptied = (sem(n) for n in ("st_filled", "exp_done", "pv_done", "pv_emptied"))
        max_split = sem("max_split")
        filled = sem("filled")
        emptied = [sem(f"emptied{i}") for i in range(2)]

        def wait_emptied(eng, task):
            eng.wait_ge(emptied[JOB[task] % 2], JOB[task] // 2 + 1)

        k_split, q_split = sem("k_split"), sem("q_split")
        stats_done, rstd_done, norm_done = sem("stats_done"), sem("rstd_done"), sem("norm_done")
        ffn0_added, bo_added = sem("ffn0_added"), sem("bo_added")
        mask_set = sem("mask_set")
        w_summed, w_mean_set, w_quant = sem("w_summed"), sem("w_mean_set"), sem("w_quant")
        x_quant = sem("x_quant")
        tapped, conved, tanhed, silued = (sem(n) for n in ("tapped", "conved", "tanhed", "silued"))
        h_quant = sem("h_quant")
        v_step, g_step = sem("v_step"), sem("g_step")

        def res_writers(eng, k, t):
            layer, b = BLOCKS[k]
            if t == 0 and layer == 0:
                eng.wait_ge(x_in[min(b, 1)], 16)
            elif t == 1:
                wait_emptied(eng, ("proj_o", k, 0))
            else:
                eng.wait_ge(ffn0_added, b + 1)

        def norm_target(k, t):
            layer, _ = BLOCKS[k]
            return xq[layer] if t == 0 else (z if layer == 0 else xf)

        block = es.enter_context(nc.Block())

        @block.sync
        def _(sp):
            sp.dma_start(proj[:, :, :], projT).then_inc(proj_in, 16)
            sp.dma_start(ctx_sb[:, 0:1, :], ctxT[0:1].rearrange("b d k -> d b k")).then_inc(ctx_in[0], 16)
            sp.dma_start(cols_sb[:, :], cols).then_inc(small_in, 16)
            sp.dma_start(rows_sb[:, :, :], rows.partition_broadcast(128)).then_inc(small_in, 16)
            sp.dma_start(ctx_sb[:, 1:B, :], ctxT[1:B].rearrange("b d k -> d b k")).then_inc(ctx_in[1], 16)
            sp.wait_ge(ones16_set, 2)
            for layer, i in ((0, 0), (0, 1), (1, 0), (1, 1)):
                for half in range(2):
                    sp.dma_start(kst[layer][i][64 * half + 48:64 * half + 64, :, :], ones16[:, :]).then_inc(k_ones[2 * layer + i], 16)
            for step in range(FIRST, LAST + 1):
                for task in TASKS.get(step, []):
                    kind, k, t = task
                    if kind == "write_k":
                        sp.wait_ge(k_split, NTH[("split_k", k, 0)] + 1)
                        sp.dma_start(k_scratch[k].rearrange("p r c -> r p c"), k_parts[:, :, :]).then_inc(k_written, 16)
                    elif kind == "write_q":
                        sp.wait_ge(q_split, NTH[("split_q", k, 0)] + 1)
                        for part, (lo, n) in enumerate(((0, 3), (3, 2), (5, 1))):
                            sp.dma_start(q_scratch[k, lo:lo + n].rearrange("p r c -> r p c"),
                                         q_parts[:, part:part + 1, :].broadcast_to([128, n, S])).then_inc(q_written, 16)
                    elif kind == "read_k":
                        layer, b = BLOCKS[k]
                        old = AT_BLOCK.get((layer, b - 2))
                        if old is not None:
                            sp.wait_ge(st_filled, 2 * PER_BLOCK * (old + 1))
                        sp.wait_ge(k_written, 16 * (NTH[("write_k", k, 0)] + 1))
                        for half in range(2):
                            for lo, n in ((0, 3), (3, 2), (5, 1)):
                                row = 64 * half + DH * lo
                                src = k_scratch[k, 0:n].rearrange("p (d h) c -> (p d) h c", d=DH)
                                sp.dma_start(kst[layer][b % 2][row:row + DH * n, :, :],
                                             src[:, 8 * half:8 * half + 8, :]).then_inc(kq_read[k], 16)
                    elif kind == "read_q":
                        layer, b = BLOCKS[k]
                        old = AT_BLOCK.get((layer, b - 2))
                        if old is not None:
                            sp.wait_ge(st_filled, 2 * PER_BLOCK * (old + 1))
                        sp.wait_ge(q_written, 48 * (NTH[("write_q", k, 0)] + 1))
                        for half in range(2):
                            heads = slice(8 * half, 8 * half + 8)
                            sp.dma_start(qst[layer][b % 2][64 * half:64 * half + 48, heads, :],
                                         q_scratch[k].rearrange("p (d h) c -> (p d) h c", d=DH)[:, heads, :]).then_inc(kq_read[k], 16)
                            sp.dma_start(qst[layer][b % 2][64 * half + 48:64 * half + 64, heads, :], zeros16[:, :]).then_inc(kq_read[k], 16)
                    elif kind == "max_t":
                        layer, b = BLOCKS[k // NJ]
                        j = k % NJ
                        wait_emptied(sp, task)
                        for part in range(2):
                            row = 64 * (HG * j // 8) + 6 * DH + part
                            sp.dma_start(qst[layer][b % 2][row:row + 1, HG * j:HG * j + HG, :],
                                         max_rows[k % 2][HG * part:HG * part + HG, :]).then_inc(max_placed[k % 2], 16)
                    elif kind == "store":
                        _, b = BLOCKS[k]
                        wait_emptied(sp, ("down", k, 0))
                        sp.dma_start(out[b].rearrange("(t p) d -> p t d", p=128), y_out[:, :, :]).then_inc(stored, 16)
            sp.wait_ge(stored, 16 * B)

        @block.gpsimd
        def _(pool):
            chain = [0]

            def link(ins):
                chain[0] += 1
                ins.then_inc(g_step, 1)
                pool.wait_ge(g_step, chain[0])

            nc.gpsimd.memset(ones16[:, :], 1.0).then_inc(ones16_set, 1)
            nc.gpsimd.memset(zeros16[:, :], 0.0).then_inc(ones16_set, 1)
            nc.gpsimd.memset(id32[:, :], 0.0).then_inc(g_step, 1)
            nc.gpsimd.memset(ones[:, :], 1.0).then_inc(ones_set, 1)
            nc.gpsimd.memset(neghalf[:, :], -0.5).then_inc(ones_set, 1)
            pool.wait_ge(g_step, 1)
            chain[0] = 1
            link(nc.gpsimd.affine_select(out=id32[:, :], in_=id32[:, :], compare_op=ALU.not_equal, fill=1.0,
                                         base=0, pattern=[[-1, 128]], channel_multiplier=1))
            nc.gpsimd.tensor_copy(id16[:, :], id32[:, :]).then_inc(id_set, 1)
            pool.wait_ge(id_set, 1)
            pool.wait_ge(ones_set, 2)
            for n, (layer, i, half) in enumerate((l, i, h) for l in range(2) for i in range(2) for h in range(2)):
                other = qst[layer][i][64 * (1 - half):64 * (1 - half) + 64, 8 * half:8 * half + 8, :]
                nc.gpsimd.memset(other.rearrange("p h c -> p (h c)").bitcast(f32), 0.0).then_inc(q_zeros, 1)
                pool.wait_ge(q_zeros, n + 1)
            for i in range(2):
                link(nc.gpsimd.memset(vst[1][i][:, :, :, :].rearrange("p t h d -> p (t h d)"), 0.0))
                nc.gpsimd.memset(vst[1][i][:, :, :, DH:DH + 1], 1.0).then_inc(v1_set, 1)
            nc.gpsimd.memset(hid[:, :, :], 0.0).then_inc(hid_set, 1)

            def split(src, rest, parts, done):
                link(nc.gpsimd.tensor_tensor(rest[:, :], src[:, :], parts[:, 0, :], ALU.subtract))
                link(nc.gpsimd.tensor_copy(parts[:, 1, :], rest[:, :]))
                nc.gpsimd.tensor_tensor(parts[:, 2, :], rest[:, :], parts[:, 1, :], ALU.subtract).then_inc(done, 1)

            for step in range(FIRST, LAST + 1):
                for task in TASKS.get(step, []):
                    kind, k, t = task
                    if kind == "split_k":
                        wait_emptied(pool, ("proj_k", k, 0))
                        split(k_f, k_rest, k_parts, k_split)
                    elif kind == "split_q":
                        wait_emptied(pool, ("proj_q", k, 0))
                        split(q_f, q_rest, q_parts, q_split)
                    elif kind == "split_max":
                        pool.wait_ge(max_taken, 8 * (k + 1))
                        if k >= 2:
                            pool.wait_ge(filled, JOB[("max_t", k - 2, 0)] + 1)
                        link(nc.gpsimd.tensor_scalar(neg_max[:, :, :], row_max[k % 2][:, :, :], -1.0, None, ALU.mult))
                        link(nc.gpsimd.tensor_copy(max_parts[k % 2][:, :, 0, :], neg_max[:, :, :]))
                        nc.gpsimd.tensor_tensor(max_parts[k % 2][:, :, 1, :], neg_max[:, :, :],
                                                max_parts[k % 2][:, :, 0, :], ALU.subtract).then_inc(max_split, 1)
                    elif kind == "stats":
                        pool.wait_ge(stats_done, NTH[task] + 1)
                        link(nc.gpsimd.tensor_scalar(var_eps[NTH[task] % NM][:, :], moments[NTH[task] % NM][:, :, 1], EPS, None, ALU.add))
                        nc.gpsimd.tensor_tensor(rstd[NTH[task] % NM][:, :], var_eps[NTH[task] % NM][:, :], neghalf[:, :], ALU.pow).then_inc(rstd_done, 1)
                    elif kind == "norm" and t == 2:
                        layer, b = BLOCKS[k]
                        pool.wait_ge(norm_done, NTH[task] + 1)
                        gamma = rows_sb[:, GAMMA:GAMMA + 1, :].broadcast_to([128, QT, D])
                        beta = rows_sb[:, BETA:BETA + 1, :].broadcast_to([128, QT, D])
                        link(nc.gpsimd.tensor_tensor(z[:, :, :], z[:, :, :], gamma, ALU.mult))
                        link(nc.gpsimd.tensor_tensor(z[:, :, :], z[:, :, :], beta, ALU.add))
                        nc.gpsimd.tensor_tensor(res[:, b, :, :], res[:, b, :, :], z[:, :, :], ALU.add).then_inc(ffn0_added, 1)
                    elif kind == "add_bo":
                        layer, b = BLOCKS[k]
                        if NTH[task] == 0:
                            pool.wait_ge(small_in, 32)
                        pool.wait_ge(norm_done, NTH[("norm", k, 0)] + 1)
                        bo = rows_sb[:, (BO0, BO1)[layer]:(BO0, BO1)[layer] + 1, :].broadcast_to([128, QT, D])
                        nc.gpsimd.tensor_tensor(res[:, b, :, :], res[:, b, :, :], bo, ALU.add).then_inc(bo_added, 1)
                    elif kind == "mask":
                        pool.wait_ge(mask_in, 32)
                        nc.gpsimd.tensor_scalar(mask_max[:, :, :], mask_i[:, :, :], 0.0, MASK_MAX, ALU.is_equal, ALU.mult).then_inc(mask_set, 1)
                        for i in range(2):
                            nc.gpsimd.tensor_scalar(mask_exp[:, :, i, :], maskT_i[:, :, :], 0.0, MASK_EXP, ALU.is_equal, ALU.mult).then_inc(mask_set, 1)
                    elif kind == "quant_w":
                        pool.wait_ge(w_mean_set, 1)
                        for i, (w, q) in enumerate(((w1_sb[:, :], w1_q[:, :]),
                                                    (w2_sb[:, :, :].rearrange("p c n -> p (c n)"),
                                                     w2_q[:, :, :].rearrange("p c n -> p (c n)")))):
                            link(nc.gpsimd.tensor_scalar(w_tmp, w, w_inv[:, i:i + 1], ROUND, ALU.mult, ALU.add))
                            link(nc.gpsimd.tensor_scalar(w_tmp, w_tmp, ROUND, 1.0, ALU.subtract, ALU.min))
                            ins = nc.gpsimd.tensor_scalar(q, w_tmp, -1.0, None, ALU.max)
                            if i == 0:
                                link(ins)
                        ins.then_inc(w_quant, 1)

        @block.scalar
        def _(act):
            act.dma_start(res[:, 0, :, :], x[0].rearrange("(t p) d -> p t d", p=128)).then_inc(x_in[0], 16)
            act.dma_start(res[:, 1:B, :, :].rearrange("p b t d -> p (b t) d"),
                          x[1:B].rearrange("b (t p) d -> p (b t) d", p=128)).then_inc(x_in[1], 16)
            act.dma_start(mask_i[:, :, :], mask.rearrange("(t p) k -> p t k", p=128)).then_inc(mask_in, 16)
            act.dma_start(maskT_i[:, :, :], maskT.rearrange("(t p) q -> p t q", p=128)).then_inc(mask_in, 16)
            act.dma_start(w1_sb[:, :], w1T).then_inc(ffn_in, 16)
            act.dma_start(w2_sb[:, :, :], w2T.rearrange("(c p) n -> p c n", p=128)).then_inc(ffn_in, 16)
            act.dma_start(conv_sb[:, :, :], conv.rearrange("(c p) n -> p c n", p=128)).then_inc(ffn_in, 16)
            for step in range(FIRST, LAST + 1):
                if 0 <= step < STEPS:
                    layer, _b = BLOCKS[step // PER_BLOCK]
                    for n in (2 * step, 2 * step + 1):
                        act.wait_ge(st_filled, n + 1)
                        if step >= NP and n % 2 == 0:
                            act.wait_ge(pv_done, step - NP + 1)
                        nc.scalar.activation(probs[step % NP][:, 2 * (n % 2):2 * (n % 2) + 2, :], st[n % NST][:, :, :], ACT.Exp,
                                             scale=SCALES[layer]).then_inc(exp_done, 1)
                if step > KT and step % KT == 1 and step // KT <= UNITS:
                    u = step // KT - 1
                    act.wait_ge(pv_done, KT * (u + 1))
                    if u >= NJ and u % NJ == 0:
                        act.wait_ge(filled, JOB[("out_t", u // NJ - 1, 1)] + 1)
                    nc.scalar.activation(o_raw[:, u % NJ, :], pv[:, 0:S], ACT.Copy).then_inc(pv_emptied, 1)
                for task in TASKS.get(step, []):
                    kind, k, t = task
                    if task in JOB:
                        bank = JOB[task] % 2
                        side, side16 = sides[bank], sides16[bank]
                    if kind in ("proj_k", "x_t", "proj_q", "proj_v", "heads_t", "xq_t", "spread_scale", "hid_t", "hq_t", "max_t"):
                        act.wait_ge(filled, JOB[task] + 1)
                    if kind == "proj_k":
                        layer, b = BLOCKS[k]
                        if NTH[task]:
                            act.wait_ge(k_split, NTH[task])
                            act.wait_ge(k_written, 16 * NTH[task])
                        for dst in (k_parts[:, 0, :], k_f[:, :]):
                            if layer == 0:
                                ins = nc.scalar.activation(dst, side[:, :], ACT.Copy)
                            else:
                                ins = nc.scalar.activation(dst, side[:, :], ACT.Identity, bias=cols_sb[:, 1:2])
                        ins.then_inc(emptied[bank], 1)
                    elif kind == "proj_q":
                        layer, b = BLOCKS[k]
                        if NTH[task]:
                            act.wait_ge(q_split, NTH[task])
                            act.wait_ge(q_written, 48 * NTH[task])
                        for dst in (q_parts[:, 0, :], q_f[:, :]):
                            if layer == 0:
                                ins = nc.scalar.activation(dst, side[:, 0:S], ACT.Copy)
                            else:
                                ins = nc.scalar.activation(dst, side[:, 0:S], ACT.Identity, bias=cols_sb[:, 0:1])
                        ins.then_inc(emptied[bank], 1)
                    elif kind == "proj_v":
                        layer, b = BLOCKS[k]
                        old = AT_BLOCK.get((layer, b - 2))
                        if old is not None:
                            act.wait_ge(pv_done, PER_BLOCK * (old + 1))
                        if old is None:
                            act.wait_ge((v_set, v1_set)[layer], 1 + b)
                        nc.scalar.activation(vst[layer][b % 2][:, :, :, 0:DH],
                                             side[:, :].rearrange("p (t h d) -> p t h d", t=KT, h=H), ACT.Copy).then_inc(emptied[bank], 1)
                    elif kind == "x_t":
                        nc.scalar.activation(x_t[:, :], side[:, 0:S], ACT.Copy).then_inc(emptied[bank], 1)
                    elif kind == "heads_t":
                        nc.scalar.activation(o_t[:, :], side[:, 0:S], ACT.Copy).then_inc(emptied[bank], 1)
                    elif kind == "xq_t":
                        nc.scalar.activation(a_t[:, :], side16[:, 0:S], ACT.Copy).then_inc(emptied[bank], 1)
                    elif kind == "spread_scale":
                        nc.scalar.activation(back_rows[:, :], side[:, 0:S], ACT.Copy).then_inc(emptied[bank], 1)
                    elif kind == "hq_t":
                        nc.scalar.activation(h_t[:, t, :, :].rearrange("p c n -> p (c n)"), side16[:, 0:HID], ACT.Copy).then_inc(emptied[bank], 1)
                    elif kind == "max_t":
                        if k >= 2:
                            act.wait_ge(max_placed[k % 2], 32 * (k // 2))
                        nc.scalar.activation(max_rows[k % 2][:, :], side16[0:2 * HG, 0:S], ACT.Copy).then_inc(emptied[bank], 1)
                    elif kind == "conv":
                        wait_emptied(act, ("up", k, 1))
                        if NTH[task]:
                            act.wait_ge(filled, JOB[[q for q in JOB if q[0] == "hid_t"][2 * NTH[task] - 1]] + 1)
                        for c in range(CH):
                            nc.scalar.activation(y[:, c, :], hid[:, c, 1:S + 1], ACT.Identity, bias=conv_sb[:, c, 3:4],
                                                 scale=conv_sb[:, c, 1:2]).then_inc(tapped, 1)
                    elif kind == "silu":
                        act.wait_ge(conved, NTH[task] + 1)
                        nc.scalar.activation(tanh_y[:, :, :], y[:, :, :], ACT.Tanh, scale=0.5).then_inc(tanhed, 1)
                    elif kind == "hid_t":
                        if NTH[task] >= QT:
                            act.wait_ge(h_quant, NTH[task] - QT + 1)
                        nc.scalar.activation(h_tmp[:, t, :], side[:, :], ACT.Copy).then_inc(emptied[bank], 1)

        @block.vector
        def _(dve):
            chain = [0]

            def link(ins):
                chain[0] += 1
                ins.then_inc(v_step, 1)
                dve.wait_ge(v_step, chain[0])

            def clear_v(layer, i):
                link(nc.vector.memset(vst[layer][i][:, :, :, :].rearrange("p t h d -> p (t h d)"), 0.0))
                nc.vector.memset(vst[layer][i][:, :, :, DH:DH + 1], 1.0).then_inc(v_set, 1)

            clear_v(0, 0)
            clear_v(0, 1)
            for step in range(FIRST, LAST + 1):
                u = step // KT + LEAD
                if 0 <= u < UNITS:
                    layer, _b = BLOCKS[u // NJ]
                    for n in (2 * (step % KT), 2 * (step % KT) + 1):
                        count = 8 * u + n
                        if u >= 2 and n == 0:
                            dve.wait_ge(max_split, u - 1)
                        if layer == 1 and u // NJ == AT_BLOCK[(1, 0)] and n == 0:
                            dve.wait_ge(mask_set, 1)
                        dve.wait_ge(sm_filled, count + 1)
                        m_out = row_max[u % 2][:, n // HG, n % HG:n % HG + 1]
                        if layer == 0:
                            nc.vector.tensor_reduce(m_out, sm[count % 2][:, :], X, ALU.max).then_inc(max_taken, 1)
                        else:
                            dve.wait_ge(max_taken, count - 1)
                            nc.vector.tensor_tensor_reduce(masked[:, n % 2, :], sm[count % 2][:, :], mask_max[:, n // HG, :],
                                                           1.0, MASK_EXP, ALU.add, ALU.max, m_out).then_inc(max_taken, 1)
                for task in TASKS.get(step, []):
                    kind, k, t = task
                    if task in JOB:
                        bank = JOB[task] % 2
                        side = sides[bank]
                    if kind == "stats":
                        layer, b = BLOCKS[k]
                        src = z if (layer == 0 and t == 2) else res[:, b, :, :]
                        if layer == 0 and t == 2:
                            dve.wait_ge(norm_done, NTH[("norm", k, 1)] + 1)
                        else:
                            res_writers(dve, k, t)
                        m = NTH[task] % NM
                        if NTH[task] >= NM:
                            dve.wait_ge(norm_done, NTH[task] - NM + 1)
                        for i in range(QT):
                            ins = nc.vector.bn_stats(bn[m][:, i, :], src[:, i, :])
                        link(ins)
                        for i in range(QT):
                            ins = nc.vector.bn_aggr(moments[m][:, i, :], bn[m][:, i, :])
                        ins.then_inc(stats_done, 1)
                    elif kind == "norm":
                        layer, b = BLOCKS[k]
                        dst, m = norm_target(k, t), NTH[task] % NM
                        src = z if (layer == 0 and t == 2) else res[:, b, :, :]
                        dve.wait_ge(rstd_done, NTH[task] + 1)
                        if t == 0:
                            before = [q for q in JOB if q[0] == "x_t" and BLOCKS[q[1]][0] == layer and NTH[q] < NTH[("x_t", k, 0)]]
                            if before:
                                dve.wait_ge(filled, JOB[before[-1]] + 1)
                        if layer == 0 and t == 1 and b:
                            dve.wait_ge(ffn0_added, b)
                        for i in range(QT):
                            ins = nc.vector.tensor_scalar(dst[:, i, :], src[:, i, :], moments[m][:, i, 0:1], rstd[m][:, i:i + 1],
                                                          ALU.subtract, ALU.mult)
                        ins.then_inc(norm_done, 1)
                    elif kind == "out_t":
                        dve.wait_ge(filled, JOB[task] + 1)
                        if NTH[task] >= QT and t == 0:
                            dve.wait_ge(filled, JOB[[q for q in JOB if q[0] == "heads_t"][NTH[task] // QT - 1]] + 1)
                        o_nat = side[:, :].rearrange("p (j g c) -> p j g c", j=NJ, g=HG)
                        link(nc.vector.reciprocal(inv_den[:, :, :], o_nat[:, :, :, DH]))
                        nc.vector.tensor_tensor(o_heads[:, t, :, :],
                                                side[:, :].rearrange("p (h c) -> p h c", h=H)[:, :, 0:DH],
                                                inv_den[:, :, :].rearrange("p j g -> p (j g)").unsqueeze(2).broadcast_to([128, H, DH]),
                                                ALU.mult).then_inc(emptied[bank], 1)
                    elif kind == "proj_o":
                        layer, b = BLOCKS[k]
                        dve.wait_ge(filled, JOB[task] + 1)
                        dve.wait_ge(bo_added, NTH[("add_bo", k, 0)] + 1)
                        flat = res[:, b, :, :].rearrange("p t d -> p (t d)")
                        nc.vector.tensor_tensor(flat, side[:, 0:S], flat, ALU.add).then_inc(emptied[bank], 1)
                    elif kind == "weight_mean":
                        dve.wait_ge(ffn_in, 48)
                        nc.vector.tensor_reduce(w_sum[:, 0:1], w1_sb[:, :], X, ALU.add, apply_absolute_value=True).then_inc(w_summed, 1)
                        nc.vector.tensor_reduce(w_sum[:, 1:2], w2_sb[:, :, :].rearrange("p c n -> p (c n)"), X, ALU.add,
                                                apply_absolute_value=True).then_inc(w_summed, 1)
                        dve.wait_ge(filled, JOB[task] + 1)
                        nc.vector.tensor_scalar(w_mean[:, :], side[:, 0:2], 1.0 / (D * HID), EPS, ALU.mult, ALU.max).then_inc(emptied[bank], 1)
                        wait_emptied(dve, task)
                        nc.vector.reciprocal(w_inv[:, :], w_mean[:, :]).then_inc(w_mean_set, 1)
                    elif kind == "quant_x":
                        dve.wait_ge(norm_done, NTH[("norm", k, 1)] + 1)
                        if NTH[task]:
                            dve.wait_ge(filled, JOB[[q for q in JOB if q[0] == "spread_scale"][NTH[task] - 1]] + 1)
                        link(nc.vector.tensor_reduce(amax[:, :], xf[:, :, :], X, ALU.max, apply_absolute_value=True))
                        link(nc.vector.tensor_scalar(amax[:, :], amax[:, :], EPS, None, ALU.max))
                        link(nc.vector.reciprocal(a_inv[:, :], amax[:, :]))
                        nc.vector.tensor_scalar(a_back[:, :], amax[:, :], w_mean[:, 0:1], 1.0 / 127.0, ALU.mult, ALU.mult)
                        link(nc.vector.tensor_scalar(a_scale[:, :], a_inv[:, :], 127.0, None, ALU.mult))
                        for i in range(QT):
                            ins = nc.vector.tensor_scalar(a_tmp[:, i, :], xf[:, i, :], a_scale[:, i:i + 1], ROUND, ALU.mult, ALU.add)
                        link(ins)
                        nc.vector.tensor_scalar(a_q[:, :, :], a_tmp[:, :, :], ROUND, None, ALU.subtract).then_inc(x_quant, 1)
                        for i in range(QT):
                            ins = nc.vector.tensor_scalar(back_diag[:, i, :], id32[:, :], a_back[:, i:i + 1], None, ALU.mult)
                        ins.then_inc(x_quant, 1)
                    elif kind == "up":
                        dve.wait_ge(filled, JOB[task] + 1)
                        if t == 0:
                            wait_emptied(dve, ("spread_scale", k, 0))
                            if NTH[task] == 0:
                                dve.wait_ge(hid_set, 1)
                            else:
                                dve.wait_ge(tapped, CH * (NTH[task] // 2))
                        nc.vector.tensor_tensor(hid[:, 2 * t:2 * t + 2, 1:S + 1],
                                                side[:, :].rearrange("p (c s) -> p c s", c=2),
                                                back_rows[:, :].unsqueeze(1).broadcast_to([128, 2, S]), ALU.mult).then_inc(emptied[bank], 1)
                    elif kind == "conv":
                        for c in range(CH):
                            dve.wait_ge(tapped, CH * NTH[task] + c + 1)
                            link(nc.vector.scalar_tensor_tensor(y[:, c, :], hid[:, c, 0:S], conv_sb[:, c, 0:1], y[:, c, :],
                                                                ALU.mult, ALU.add))
                            ins = nc.vector.scalar_tensor_tensor(y[:, c, :], hid[:, c, 2:S + 2], conv_sb[:, c, 2:3], y[:, c, :],
                                                                 ALU.mult, ALU.add)
                        ins.then_inc(conved, 1)
                    elif kind == "silu":
                        dve.wait_ge(tanhed, NTH[task] + 1)
                        flat = [a[:, :, :].rearrange("p c s -> p (c s)") for a in (tanh_y, y)]
                        nc.vector.scalar_tensor_tensor(flat[1], flat[0], 1.0, flat[1], ALU.add, ALU.mult).then_inc(silued, 1)
                    elif kind == "quant_h":
                        wait_emptied(dve, ("hid_t", k, t))
                        if NTH[task] >= QT:
                            dve.wait_ge(filled, JOB[[q for q in JOB if q[0] == "hq_t"][NTH[task] - QT]] + 1)
                        m, inv, row = h_max[:, t:t + 1], h_inv[:, t:t + 1], h_tmp[:, t, :]
                        link(nc.vector.tensor_reduce(m, row, X, ALU.max, apply_absolute_value=True))
                        link(nc.vector.tensor_scalar(m, m, 2 * EPS, None, ALU.max))
                        link(nc.vector.reciprocal(inv, m))
                        nc.vector.tensor_scalar(h_back[:, t:t + 1], m, w_mean[:, 1:2], 0.5 / 127.0, ALU.mult, ALU.mult)
                        link(nc.vector.tensor_scalar(h_scale[:, t:t + 1], inv, 127.0, None, ALU.mult))
                        link(nc.vector.tensor_scalar(row, row, h_scale[:, t:t + 1], ROUND, ALU.mult, ALU.add))
                        nc.vector.tensor_scalar(h_q[:, t, :], row, ROUND, None, ALU.subtract).then_inc(h_quant, 1)
                    elif kind == "down":
                        _, b = BLOCKS[k]
                        dve.wait_ge(filled, JOB[task] + 1)
                        if NTH[task]:
                            dve.wait_ge(stored, 16 * NTH[task])
                        for i in range(QT):
                            ins = nc.vector.scalar_tensor_tensor(y_out[:, i, :], side[:, 128 * i:128 * i + 128], h_back[:, i:i + 1],
                                                                 res[:, b, i, :], ALU.mult, ALU.add)
                        ins.then_inc(emptied[bank], 1)

        @block.tensor
        def _(pe):
            def scores_t(step):
                k, j, kt = step // PER_BLOCK, step // KT % NJ, step % KT
                layer, b = BLOCKS[k]
                ks, qs, u = kst[layer][b % 2], qst[layer][b % 2], step // KT
                if kt == 0:
                    pe.wait_ge(max_placed[u % 2], 32 * (u // 2 + 1))
                for g in range(HG):
                    n = 2 * step + g // 2
                    if g % 2 == 0 and n >= NST:
                        pe.wait_ge(exp_done, n - NST + 1)
                    if layer == 1 and g % 2 == 0:
                        if step == PER_BLOCK * AT_BLOCK[(1, 0)] and g == 0:
                            pe.wait_ge(mask_set, 3)
                        nc.tensor.matmul(st[n % NST][:, :, :], id16[:, :], mask_exp[:, kt, :, :], start=True, stop=False)
                    h = HG * j + g
                    ins = nc.tensor.matmul(st[n % NST][:, g % 2, :], ks[:, h % 8, 128 * kt:128 * kt + 128], qs[:, h, :],
                                           start=layer == 0, stop=layer == 0 or g % 2 == 1)
                    if g % 2 == 1:
                        ins.then_inc(st_filled, 1)

            def scores(u, n):
                k, j, t, g = u // NJ, u % NJ, n // HG, n % HG
                layer, b = BLOCKS[k]
                count = 8 * u + n
                if j == 0 and n == 0:
                    pe.wait_ge(kq_read[k], 160)
                    if b < 2:
                        pe.wait_ge(k_ones[2 * layer + b], 32)
                        pe.wait_ge(q_zeros, 4 * layer + 2 * b + 2)
                if count >= 2:
                    pe.wait_ge(max_taken, count - 1)
                h = HG * j + g
                nc.tensor.matmul(sm[count % 2][:, :], qst[layer][b % 2][:, h, 128 * t:128 * t + 128],
                                 kst[layer][b % 2][:, h % 8, :], start=True, stop=True).then_inc(sm_filled, 1)

            def weighted(step):
                k, j, kt = step // PER_BLOCK, step // KT % NJ, step % KT
                layer, b = BLOCKS[k]
                if step % PER_BLOCK == 0:
                    wait_emptied(pe, ("proj_v", k, 0))
                if kt == 0 and step:
                    pe.wait_ge(pv_emptied, step // KT)
                pe.wait_ge(exp_done, 2 * step + 2)
                for g in range(HG):
                    ins = nc.tensor.matmul(pv[32 * g:32 * g + 32, 0:S], vst[layer][b % 2][:, kt, HG * j + g, :],
                                           probs[step % NP][:, g, :], start=kt == 0, stop=kt == KT - 1)
                ins.then_inc(pv_done, 1)

            def job(task):
                kind, k, t = task
                n = JOB[task]
                side, side16 = sides[n % 2], sides16[n % 2]
                if n >= 2:
                    pe.wait_ge(emptied[n % 2], n // 2)
                if kind == "proj_k":
                    layer, b = BLOCKS[k]
                    if NTH[task] == 0:
                        pe.wait_ge(proj_in, 16)
                    pe.wait_ge(ctx_in[min(b, 1)], 16)
                    if NTH[task] == 0:
                        pe.wait_ge(small_in, 32)
                    ins = nc.tensor.matmul(side[:, :], proj[:, 4 * layer + 1, :], ctx_sb[:, b, :], start=True, stop=True)
                elif kind == "proj_v":
                    layer, b = BLOCKS[k]
                    for i in range(KT):
                        sl = side[:, 128 * i:128 * i + 128]
                        ins = nc.tensor.matmul(sl, ctx_sb[:, b, 128 * i:128 * i + 128], proj[:, 4 * layer + 2, :],
                                               start=True, stop=layer == 0)
                        if layer == 1:
                            ins = nc.tensor.matmul(sl, ones[0:1, :], rows_sb[0:1, BV1, :], start=False, stop=True)
                elif kind == "x_t":
                    layer, b = BLOCKS[k]
                    pe.wait_ge(norm_done, NTH[("norm", k, 0)] + 1)
                    if NTH[task] == 0:
                        pe.wait_ge(id_set, 1)
                    for i in range(QT):
                        ins = nc.tensor.transpose(side[:, 128 * i:128 * i + 128], xq[layer][:, i, :], id32[:, :])
                elif kind == "proj_q":
                    layer, b = BLOCKS[k]
                    wait_emptied(pe, ("x_t", k, 0))
                    ins = nc.tensor.matmul(side[:, 0:S], proj[:, 4 * layer, :], x_t[:, :], start=True, stop=True)
                elif kind == "max_t":
                    pe.wait_ge(max_split, k + 1)
                    for i in range(QT):
                        ins = nc.tensor.transpose(side16[0:2 * HG, 128 * i:128 * i + 128],
                                                  max_parts[k % 2][:, i, :, :].rearrange("p a g -> p (a g)"), id16[:, :])
                elif kind == "out_t":
                    pe.wait_ge(pv_emptied, NJ * (k + 1))
                    for j in range(NJ):
                        ins = nc.tensor.transpose(side[:, 128 * j:128 * j + 128], o_raw[:, j, 128 * t:128 * t + 128], id32[:, :])
                elif kind == "heads_t":
                    wait_emptied(pe, ("out_t", k, 1))
                    for i in range(QT):
                        ins = nc.tensor.transpose(side[:, 128 * i:128 * i + 128],
                                                  o_heads[:, i, :, :].rearrange("p h d -> p (h d)"), id32[:, :])
                elif kind == "proj_o":
                    layer, b = BLOCKS[k]
                    wait_emptied(pe, ("heads_t", k, 0))
                    for i in range(QT):
                        ins = nc.tensor.matmul(side[:, 128 * i:128 * i + 128], o_t[:, 128 * i:128 * i + 128],
                                               proj[:, 4 * layer + 3, :], start=True, stop=True)
                elif kind == "weight_mean":
                    pe.wait_ge(w_summed, 2)
                    pe.wait_ge(ones_set, 1)
                    ins = nc.tensor.matmul(side[:, 0:2], ones[:, :], w_sum[:, :], start=True, stop=True)
                elif kind == "xq_t":
                    pe.wait_ge(x_quant, 2 * NTH[task] + 1)
                    for i in range(QT):
                        ins = nc.tensor.transpose(side16[:, 128 * i:128 * i + 128], a_q[:, i, :], id16[:, :])
                elif kind == "spread_scale":
                    pe.wait_ge(x_quant, 2 * NTH[task] + 2)
                    ins = nc.tensor.matmul(side[:, 0:S], ones[:, :], back_diag[:, :, :].rearrange("p t s -> p (t s)"),
                                           start=True, stop=True)
                elif kind == "up":
                    if t == 0:
                        wait_emptied(pe, ("xq_t", k, 0))
                        if NTH[task] == 0:
                            pe.wait_ge(w_quant, 1)
                    for i in range(2):
                        c = 2 * t + i
                        ins = nc.tensor.matmul(side[:, S * i:S * i + S], w1_q[:, 128 * c:128 * c + 128], a_t[:, :],
                                               start=True, stop=True)
                elif kind == "hid_t":
                    pe.wait_ge(silued, NTH[("silu", k, 0)] + 1)
                    for c in range(CH):
                        ins = nc.tensor.transpose(side[:, 128 * c:128 * c + 128], y[:, c, 128 * t:128 * t + 128], id32[:, :])
                elif kind == "hq_t":
                    pe.wait_ge(h_quant, NTH[("quant_h", k, t)] + 1)
                    for c in range(CH):
                        ins = nc.tensor.transpose(side16[:, 128 * c:128 * c + 128], h_q[:, t, 128 * c:128 * c + 128], id16[:, :])
                elif kind == "down":
                    wait_emptied(pe, ("hq_t", k, 1))
                    for i in range(QT):
                        for c in range(CH):
                            ins = nc.tensor.matmul(side[:, 128 * i:128 * i + 128], h_t[:, i, c, :], w2_q[:, c, :],
                                                   start=c == 0, stop=c == CH - 1)
                ins.then_inc(filled, 1)

            for step in range(FIRST, LAST + 1):
                if 0 <= step + 1 < STEPS:
                    scores_t(step + 1)
                u = step // KT + LEAD
                if 0 <= u < UNITS:
                    for n in (2 * (step % KT), 2 * (step % KT) + 1):
                        scores(u, n)
                for task in TASKS.get(step, []):
                    if task in JOB:
                        job(task)
                if 2 <= step <= STEPS and step % 2 == 0:
                    weighted(step - 2)
                    weighted(step - 1)


def kernel(**inputs):
    import numpy as np
    import concourse.bacc as bacc
    from concourse.bass_utils import run_bass_kernel_spmd

    a = {name: np.asarray(value) for name, value in inputs.items()}
    by_dim = np.arange(D).reshape(H, DH).T.reshape(-1)
    arrays = {
        "x": a["x"],
        "ctxT": a["ctx_1024"].transpose(0, 2, 1),
        "projT": np.stack([
            a["L0_xattn_Wq"][by_dim].T, a["L0_xattn_Wk"][by_dim].T, a["L0_xattn_Wv"].T, a["L0_xattn_Wo"].T,
            a["L1_xattn_w_q"][by_dim].T, a["L1_xattn_w_k"][by_dim].T, a["L1_xattn_w_v"].T, a["L1_xattn_w_o"].T], axis=1),
        "rows": np.stack([a["L0_xattn_bo"], a["L0_ffn_ln_g"], a["L0_ffn_ln_b"], a["L1_xattn_b_o"], a["L1_xattn_b_v"]]),
        "cols": np.stack([a["L1_xattn_b_q"][by_dim], a["L1_xattn_b_k"][by_dim]], axis=1),
        "mask": a["mask_1x1xSxS2_ik0"][0, 0],
        "maskT": a["mask_1x1xSxS2_ik0"][0, 0].T,
        "w1T": a["L1_ffn_w1"].T,
        "conv": np.concatenate([a["L1_ffn_conv_w"][:, 0, :], a["L1_ffn_conv_b"][:, None]], axis=1),
        "w2T": a["L1_ffn_w2"].T,
    }
    arrays = {name: np.ascontiguousarray(value) for name, value in arrays.items()}
    nc = bacc.Bacc("TRN2", target_bir_lowering=False, num_devices=1)
    aps = [nc.dram_tensor(name, value.shape, mybir.dt.from_np(value.dtype), kind="ExternalInput").ap()
           for name, value in arrays.items()]
    out = nc.dram_tensor("out", (B, S, D), mybir.dt.float32, kind="ExternalOutput").ap()
    build(nc, *aps, out)
    result = run_bass_kernel_spmd(nc, [arrays], core_ids=[0])
    return result.results[0]["out"]
```

```python
import concourse.bass as bass
from concourse import mybir
from contextlib import ExitStack

B, S, D = 4, 256, 128
SK = 512
H, DH = 16, 8
HID = 512
QT, KT, CH = S // 128, SK // 128, HID // 128
HG = 4
NJ = H // HG
EPS = 1e-5
SCALES = (D ** -0.5, DH ** -0.5)
ROUND = 12582912.0
MASK_MAX, MASK_EXP = -1e30, -3e38

BLOCKS = [(0, 0), (0, 1), (0, 2), (1, 0), (0, 3), (1, 1), (1, 2), (1, 3)]
NB = len(BLOCKS)
AT_BLOCK = {lb: k for k, lb in enumerate(BLOCKS)}
UNITS = NB * NJ
STEPS = UNITS * KT
LEAD = 3
PER_BLOCK = NJ * KT
NST = 3
NM = 3
NP = 4


def schedule():
    at = {}

    def add(step, *task):
        at.setdefault(round(2 * step), []).append(task)

    for k, (layer, b) in enumerate(BLOCKS):
        s = PER_BLOCK * k - 28
        old = AT_BLOCK.get((layer, b - 2))
        free = PER_BLOCK * (old + 1) if old is not None else -99
        if layer == 0:
            add(s, "stats", k, 0)
        add(s + 1, "proj_k", k, 0)
        add(s + 1, "split_k", k, 0)
        if layer == 0:
            add(s + 1, "norm", k, 0)
        add(s + 2, "proj_k", k, 1)
        add(s + 2, "split_k", k, 1)
        if layer == 0:
            add(s + 2.5, "x_t", k, 0)
        add(s + 3, "write_k", k, 0)
        if layer == 0:
            add(s + 3.5, "proj_q", k, 0)
            add(s + 3.5, "split_q", k, 0)
            add(s + 4, "write_q", k, 0)
            add(s + 4, "add_bo", k, 0)
        add(max(s + 5, free + 1), "proj_v", k, 0)
        add(max(s + 6, free + 2), "proj_v", k, 1)
        add(max(s + 6, free), "read_k", k, 0)
        if layer == 0:
            add(max(s + 7, free), "read_q", k, 0)
        e = PER_BLOCK * (k + 1)
        add(e + 2, "out_t", k, 0)
        add(e + 2.5, "out_t", k, 1)
        add(e + 4, "heads_t", k, 0)
        add(e + 5, "proj_o", k, 0)
        add(e + 6, "stats", k, 1)
        add(e + 7, "norm", k, 1)
        if layer == 0:
            k1 = AT_BLOCK[(1, b)]
            old = AT_BLOCK.get((1, b - 2))
            free = PER_BLOCK * (old + 1) if old is not None else -99
            add(e + 8, "stats", k, 2)
            add(e + 9, "norm", k, 2)
            add(e + 11, "stats", k1, 0)
            add(e + 12, "norm", k1, 0)
            add(e + 13, "x_t", k1, 0)
            add(e + 14, "proj_q", k1, 0)
            add(e + 14, "split_q", k1, 0)
            add(e + 14, "add_bo", k1, 0)
            add(e + 15, "write_q", k1, 0)
            add(max(e + 17, free), "read_q", k1, 0)
        else:
            add(e + 8, "quant_x", k, 0)
            add(e + 9.5, "xq_t", k, 0)
            add(e + 10, "spread_scale", k, 0)
            add(e + 11, "up", k, 0)
            add(e + 11.5, "conv", k, 0)
            add(e + 12, "up", k, 1)
            add(e + 12.5, "conv", k, 1)
            add(e + 13.5, "silu", k, 0)
            add(e + 14.5, "silu", k, 1)
            add(e + 16, "hid_t", k, 0)
            add(e + 17, "hid_t", k, 1)
            add(e + 17, "quant_h", k, 0)
            add(e + 18, "quant_h", k, 1)
            add(e + 19, "hq_t", k, 0)
            add(e + 20, "hq_t", k, 1)
            add(e + 21, "down", k, 0)
            add(e + 22, "store", k, 0)
    for u in range(UNITS):
        add(KT * (u - LEAD + 1), "split_max", u, 0)
        add(KT * (u - LEAD + 1) + 2, "max_t", u, 0)
    add(-24, "load_rest", 0, 0)
    add(-23, "clear", 0, 0)
    add(-6, "clear", 1, 0)
    add(-20, "mask", 0, 0)
    add(-19, "weight_mean", 0, 0)
    add(-18, "quant_w", 0, 0)
    return at


TASKS = schedule()
FIRST, LAST = min(TASKS), max(max(TASKS), 2 * STEPS)
ORDER = [task for half in range(FIRST, LAST + 1) for task in TASKS.get(half, [])]
JOBS = ("proj_k", "x_t", "proj_q", "proj_v", "out_t", "heads_t", "proj_o", "xq_t", "spread_scale", "up",
        "hid_t", "hq_t", "down", "max_t", "weight_mean")
JOB = {task: n for n, task in enumerate(t for t in ORDER if t[0] in JOBS)}
NTH = {}
for _task in ORDER:
    NTH[_task] = sum(1 for t in NTH if t[0] == _task[0])


def build(nc, x, ctxT, projT, rows, cols, mask, maskT, w1T, conv, w2T, out):
    f32, bf16, i32 = mybir.dt.float32, mybir.dt.bfloat16, mybir.dt.int32
    ALU = mybir.AluOpType
    ACT = mybir.ActivationFunctionType
    X = mybir.AxisListType.X
    BO0, GAMMA, BETA, BO1, BV1 = range(5)

    k_scratch = nc.dram_tensor("k_scratch", [NB, 3, 128, SK], bf16).ap()
    q_scratch = nc.dram_tensor("q_scratch", [NB, 6, 128, S], bf16).ap()

    es = ExitStack()
    with es:
        def sb(name, shape, dt=f32):
            return es.enter_context(nc.sbuf_tensor(name, shape, dt))

        def sem(name):
            return es.enter_context(nc.semaphore(name))

        res = sb("res", [128, B, QT, D])
        ctx_sb = sb("ctx_sb", [128, B, SK])
        proj = sb("proj", [128, 8, D])
        rows_sb = sb("rows_sb", [128, 5, D])
        cols_sb = sb("cols_sb", [128, 2])
        mask_i = sb("mask_i", [128, QT, SK], i32)
        maskT_i = sb("maskT_i", [128, KT, S], i32)
        w1_sb = sb("w1_sb", [128, HID])
        w2_sb = sb("w2_sb", [128, CH, D])
        conv_sb = sb("conv_sb", [128, CH, 4])
        id32 = sb("id32", [128, 128])
        id16 = sb("id16", [128, 128], bf16)
        ones = sb("ones", [128, 128])
        minus16 = sb("minus16", [128, 512], bf16)
        zeros16 = sb("zeros16", [128, 256], bf16)
        neghalf = sb("neghalf", [128, QT])
        kst = [[sb(f"kst{l}{i}", [128, H // 2, SK], bf16) for i in range(2)] for l in range(2)]
        qst = [[sb(f"qst{l}{i}", [128, H, S], bf16) for i in range(2)] for l in range(2)]
        vst = [[sb(f"vst{l}{i}", [128, KT, H, 32]) for i in range(2)] for l in range(2)]
        mask_max = sb("mask_max", [128, QT, SK])
        mask_exp = sb("mask_exp", [128, KT, 2, S], bf16)
        masked = sb("masked", [128, 2, SK], bf16)
        k_f = sb("k_f", [128, SK])
        k_rest = sb("k_rest", [128, SK])
        k_parts = sb("k_parts", [128, 3, SK], bf16)
        q_f = sb("q_f", [128, S])
        q_rest = sb("q_rest", [128, S])
        q_parts = sb("q_parts", [128, 3, S], bf16)
        row_max = [sb(f"row_max{i}", [128, QT, HG]) for i in range(2)]
        max_parts = [sb(f"max_parts{i}", [128, QT, 2, HG], bf16) for i in range(2)]
        max_rows = [sb(f"max_rows{i}", [2 * HG, S], bf16) for i in range(2)]
        probs = [sb(f"probs{i}", [128, HG, S]) for i in range(NP)]
        o_raw = sb("o_raw", [128, NJ, S])
        inv_den = sb("inv_den", [128, QT, NJ, HG])
        o_heads = sb("o_heads", [128, QT, H, DH])
        o_t = sb("o_t", [128, S])
        bn = [sb(f"bn{i}", [128, QT, 6]) for i in range(NM)]
        moments = [sb(f"moments{i}", [128, QT, 2]) for i in range(NM)]
        var_eps = [sb(f"var_eps{i}", [128, QT]) for i in range(NM)]
        rstd = [sb(f"rstd{i}", [128, QT]) for i in range(NM)]
        xq = [sb(f"xq{l}", [128, QT, D]) for l in range(2)]
        z = sb("z", [128, QT, D])
        xf = sb("xf", [128, QT, D])
        x_t = sb("x_t", [128, S])
        w_sum = sb("w_sum", [128, 2])
        w_mean = sb("w_mean", [128, 2])
        w_inv = sb("w_inv", [128, 2])
        w1_q = sb("w1_q", [128, HID], bf16)
        w2_q = sb("w2_q", [128, CH, D], bf16)
        amax = sb("amax", [128, QT])
        a_inv = sb("a_inv", [128, QT])
        a_scale = sb("a_scale", [128, QT])
        a_back = sb("a_back", [128, QT])
        a_tmp = sb("a_tmp", [128, QT, D])
        a_q = sb("a_q", [128, QT, D], bf16)
        back_diag = sb("back_diag", [128, QT, 128])
        a_t = sb("a_t", [128, S], bf16)
        back_rows = sb("back_rows", [128, S])
        hid = sb("hid", [128, CH, S + 2])
        y = sb("y", [128, CH, S])
        w_tmp = y[:, 0:2, :].rearrange("p c s -> p (c s)")
        tanh_y = sb("tanh_y", [128, CH, S])
        h_max = sb("h_max", [128, QT])
        h_inv = sb("h_inv", [128, QT])
        h_scale = sb("h_scale", [128, QT])
        h_back = sb("h_back", [128, QT])
        h_tmp = sb("h_tmp", [128, QT, HID])
        h_q = sb("h_q", [128, QT, HID], bf16)
        h_t = sb("h_t", [128, QT, CH, 128], bf16)
        y_out = sb("y_out", [128, QT, D])

        st = [es.enter_context(nc.psum_tensor(f"st{i}", [128, 2, S], f32)) for i in range(NST)]
        sm = [es.enter_context(nc.psum_tensor(f"sm{i}", [128, SK], f32)) for i in range(2)]
        pv = es.enter_context(nc.psum_tensor("pv", [128, 512], f32))
        sides = [es.enter_context(nc.psum_tensor(f"side{i}", [128, 512], f32)) for i in range(2)]
        sides16 = [a[:, :].bitcast(bf16) for a in sides]

        x_in = [sem(f"x_in{i}") for i in range(2)]
        ctx_in = [sem(f"ctx_in{i}") for i in range(2)]
        proj_in = [sem(f"proj_in{i}") for i in range(2)]
        small_in = sem("small_in")
        mask_in = sem("mask_in")
        ffn_in = sem("ffn_in")
        k_written, q_written = sem("k_written"), sem("q_written")
        kq_read = [sem(f"kq_read{k}") for k in range(NB)]
        max_placed = [sem(f"max_placed{i}") for i in range(2)]
        stored = sem("stored")
        id_set, ones_set, minus16_set, hid_set = (
            sem(n) for n in ("id_set", "ones_set", "minus16_set", "hid_set"))
        k_ones = [sem(f"k_ones{i}") for i in range(4)]
        q_zeros = sem("q_zeros")
        v_set = [[sem(f"v_set{l}{i}") for i in range(2)] for l in range(2)]
        sm_filled, max_taken = sem("sm_filled"), sem("max_taken")
        st_filled, exp_done, pv_done, pv_emptied = (sem(n) for n in ("st_filled", "exp_done", "pv_done", "pv_emptied"))
        max_split = sem("max_split")
        filled = sem("filled")
        emptied = [sem(f"emptied{i}") for i in range(2)]

        def wait_emptied(eng, task):
            eng.wait_ge(emptied[JOB[task] % 2], JOB[task] // 2 + 1)

        k_split, q_split = sem("k_split"), sem("q_split")
        stats_done, rstd_done, norm_done = sem("stats_done"), sem("rstd_done"), sem("norm_done")
        ffn0_added, bo_added = sem("ffn0_added"), sem("bo_added")
        mask_set = sem("mask_set")
        w_summed, w_mean_set, w_quant = sem("w_summed"), sem("w_mean_set"), sem("w_quant")
        x_quant = sem("x_quant")
        tapped, conved, tanhed, silued = (sem(n) for n in ("tapped", "conved", "tanhed", "silued"))
        h_quant = sem("h_quant")
        v_step, g_step = sem("v_step"), sem("g_step")

        def res_writers(eng, k, t):
            layer, b = BLOCKS[k]
            if t == 0 and layer == 0:
                eng.wait_ge(x_in[min(b, 1)], 16)
            elif t == 1:
                wait_emptied(eng, ("proj_o", k, 0))
            else:
                eng.wait_ge(ffn0_added, b + 1)

        def k_split_aps(t):
            cut = slice(S * t, S * t + S)
            return k_f[:, cut], k_rest[:, cut], [k_parts[:, i, cut] for i in range(3)]

        def q_split_aps():
            return q_f[:, :], q_rest[:, :], [q_parts[:, i, :] for i in range(3)]

        def norm_target(k, t):
            layer, _ = BLOCKS[k]
            return xq[layer] if t == 0 else (z if layer == 0 else xf)

        block = es.enter_context(nc.Block())

        @block.sync
        def _(sp):
            sp.dma_start(proj[:, 0:2, :], projT[:, 0:2, :]).then_inc(proj_in[0], 16)
            sp.dma_start(ctx_sb[:, 0:1, :], ctxT[0:1].rearrange("b d k -> d b k")).then_inc(ctx_in[0], 16)
            sp.wait_ge(minus16_set, 2)

            def place_minus_ones(layer, i):
                for upper in range(2):
                    sp.dma_start(kst[layer][i][64 * upper + 48:64 * upper + 64, :, :], minus16[:, :]).then_inc(k_ones[2 * layer + i], 16)

            place_minus_ones(0, 0)
            sp.dma_start(proj[:, 2:8, :], projT[:, 2:8, :]).then_inc(proj_in[1], 16)
            sp.dma_start(mask_i[:, :, :], mask.rearrange("(t p) k -> p t k", p=128)).then_inc(mask_in, 16)
            sp.dma_start(maskT_i[:, :, :], maskT.rearrange("(t p) q -> p t q", p=128)).then_inc(mask_in, 16)
            sp.dma_start(w1_sb[:, :], w1T).then_inc(ffn_in, 16)
            sp.dma_start(w2_sb[:, :, :], w2T.rearrange("(c p) n -> p c n", p=128)).then_inc(ffn_in, 16)
            for half in range(FIRST, LAST + 1):
                for task in TASKS.get(half, []):
                    kind, k, t = task
                    if kind == "load_rest":
                        sp.dma_start(rows_sb[:, :, :], rows.partition_broadcast(128)).then_inc(small_in, 16)
                        sp.dma_start(res[:, 1:B, :, :].rearrange("p b t d -> p (b t) d"),
                                     x[1:B].rearrange("b (t p) d -> p (b t) d", p=128)).then_inc(x_in[1], 16)
                        sp.dma_start(ctx_sb[:, 1:B, :], ctxT[1:B].rearrange("b d k -> d b k")).then_inc(ctx_in[1], 16)
                        sp.dma_start(cols_sb[:, :], cols).then_inc(small_in, 16)
                        sp.dma_start(conv_sb[:, :, :], conv.rearrange("(c p) n -> p c n", p=128)).then_inc(small_in, 16)
                        for layer, i in ((0, 1), (1, 0), (1, 1)):
                            place_minus_ones(layer, i)
                    elif kind == "write_k":
                        sp.wait_ge(k_split, NTH[("split_k", k, 1)] + 1)
                        sp.dma_start(k_scratch[k].rearrange("p r c -> r p c"), k_parts[:, :, :]).then_inc(k_written, 16)
                    elif kind == "write_q":
                        wait_emptied(sp, ("proj_q", k, 0))
                        for part, (lo, n) in enumerate(((0, 3), (3, 2), (5, 1))):
                            if part:
                                sp.wait_ge(q_split, 2 * NTH[("split_q", k, 0)] + part)
                            sp.dma_start(q_scratch[k, lo:lo + n].rearrange("p r c -> r p c"),
                                         q_parts[:, part:part + 1, :].broadcast_to([128, n, S])).then_inc(q_written, 16)
                    elif kind == "read_k":
                        layer, b = BLOCKS[k]
                        old = AT_BLOCK.get((layer, b - 2))
                        if old is not None:
                            sp.wait_ge(st_filled, 2 * PER_BLOCK * (old + 1))
                        sp.wait_ge(k_written, 16 * (NTH[("write_k", k, 0)] + 1))
                        for upper in range(2):
                            for lo, n in ((0, 3), (3, 2), (5, 1)):
                                row = 64 * upper + DH * lo
                                src = k_scratch[k, 0:n].rearrange("p (d h) c -> (p d) h c", d=DH)
                                sp.dma_start(kst[layer][b % 2][row:row + DH * n, :, :],
                                             src[:, 8 * upper:8 * upper + 8, :]).then_inc(kq_read[k], 16)
                    elif kind == "read_q":
                        layer, b = BLOCKS[k]
                        old = AT_BLOCK.get((layer, b - 2))
                        if old is not None:
                            sp.wait_ge(st_filled, 2 * PER_BLOCK * (old + 1))
                        for upper in range(2):
                            sp.dma_start(qst[layer][b % 2][64 * upper + 48:64 * upper + 64, 8 * upper:8 * upper + 8, :],
                                         zeros16[:, :]).then_inc(kq_read[k], 16)
                        sp.wait_ge(q_written, 48 * (NTH[("write_q", k, 0)] + 1))
                        for upper in range(2):
                            heads = slice(8 * upper, 8 * upper + 8)
                            sp.dma_start(qst[layer][b % 2][64 * upper:64 * upper + 48, heads, :],
                                         q_scratch[k].rearrange("p (d h) c -> (p d) h c", d=DH)[:, heads, :]).then_inc(kq_read[k], 16)
                    elif kind == "max_t":
                        layer, b = BLOCKS[k // NJ]
                        j = k % NJ
                        wait_emptied(sp, task)
                        for part in range(2):
                            row = 64 * (HG * j // 8) + 6 * DH + part
                            sp.dma_start(qst[layer][b % 2][row:row + 1, HG * j:HG * j + HG, :],
                                         max_rows[k % 2][HG * part:HG * part + HG, :]).then_inc(max_placed[k % 2], 16)
                    elif kind == "store":
                        _, b = BLOCKS[k]
                        wait_emptied(sp, ("down", k, 0))
                        sp.dma_start(out[b].rearrange("(t p) d -> p t d", p=128), y_out[:, :, :]).then_inc(stored, 16)
            sp.wait_ge(stored, 16 * B)

        @block.gpsimd
        def _(pool):
            chain = [0]

            def link(ins):
                chain[0] += 1
                ins.then_inc(g_step, 1)
                pool.wait_ge(g_step, chain[0])

            nc.gpsimd.memset(minus16[:, :], -1.0).then_inc(minus16_set, 1)
            nc.gpsimd.memset(zeros16[:, :], 0.0).then_inc(minus16_set, 1)
            nc.gpsimd.memset(id32[:, :], 0.0).then_inc(g_step, 1)
            nc.gpsimd.memset(ones[:, :], 1.0).then_inc(ones_set, 1)
            nc.gpsimd.memset(neghalf[:, :], -0.5).then_inc(ones_set, 1)
            pool.wait_ge(g_step, 1)
            chain[0] = 1
            link(nc.gpsimd.affine_select(out=id32[:, :], in_=id32[:, :], compare_op=ALU.not_equal, fill=1.0,
                                         base=0, pattern=[[-1, 128]], channel_multiplier=1))
            nc.gpsimd.tensor_copy(id16[:, :], id32[:, :]).then_inc(id_set, 1)
            pool.wait_ge(id_set, 1)
            pool.wait_ge(ones_set, 2)

            def clear_q(layer, i, upper):
                other = qst[layer][i][64 * (1 - upper):64 * (1 - upper) + 64, 8 * upper:8 * upper + 8, :]
                nc.gpsimd.memset(other.rearrange("p h c -> p (h c)").bitcast(f32), 0.0).then_inc(q_zeros, 1)
                pool.wait_ge(q_zeros, 4 * layer + 2 * i + upper + 1)

            def clear_v(layer, i):
                link(nc.gpsimd.memset(vst[layer][i][:, :, :, :].rearrange("p t h d -> p (t h d)"), 0.0))
                nc.gpsimd.memset(vst[layer][i][:, :, :, DH:DH + 1], 1.0).then_inc(v_set[layer][i], 1)
                pool.wait_ge(v_set[layer][i], 1)

            clear_q(0, 0, 0)
            clear_q(0, 0, 1)

            for half in range(FIRST, LAST + 1):
                for task in TASKS.get(half, []):
                    kind, k, t = task
                    if kind == "split_k" and k > 0:
                        wait_emptied(pool, ("proj_k", k, t))
                        src, rest, parts = k_split_aps(t)
                        link(nc.gpsimd.tensor_tensor(rest, src, parts[0], ALU.subtract))
                        link(nc.gpsimd.tensor_copy(parts[1], rest))
                        nc.gpsimd.tensor_tensor(parts[2], rest, parts[1], ALU.subtract).then_inc(k_split, 1)
                    elif kind == "split_q" and k > 0:
                        wait_emptied(pool, ("proj_q", k, 0))
                        n = 2 * NTH[task]
                        src, rest, parts = q_split_aps()
                        link(nc.gpsimd.tensor_tensor(rest, src, parts[0], ALU.subtract))
                        nc.gpsimd.tensor_copy(parts[1], rest).then_inc(q_split, 1)
                        pool.wait_ge(q_split, n + 1)
                        nc.gpsimd.tensor_tensor(parts[2], rest, parts[1], ALU.subtract).then_inc(q_split, 1)
                    elif kind == "clear":
                        for i in (range(1, 2) if k == 0 else range(2)):
                            clear_v(k, i)
                            clear_q(k, i, 0)
                            clear_q(k, i, 1)
                        if k == 1:
                            nc.gpsimd.memset(hid[:, :, :], 0.0).then_inc(hid_set, 1)
                    elif kind == "split_max":
                        pool.wait_ge(max_taken, 8 * (k + 1))
                        if k >= 2:
                            pool.wait_ge(filled, JOB[("max_t", k - 2, 0)] + 1)
                        link(nc.gpsimd.tensor_copy(max_parts[k % 2][:, :, 0, :], row_max[k % 2][:, :, :]))
                        nc.gpsimd.tensor_tensor(max_parts[k % 2][:, :, 1, :], row_max[k % 2][:, :, :],
                                                max_parts[k % 2][:, :, 0, :], ALU.subtract).then_inc(max_split, 1)
                    elif kind == "stats":
                        pool.wait_ge(stats_done, NTH[task] + 1)
                        link(nc.gpsimd.tensor_scalar(var_eps[NTH[task] % NM][:, :], moments[NTH[task] % NM][:, :, 1], EPS, None, ALU.add))
                        nc.gpsimd.tensor_tensor(rstd[NTH[task] % NM][:, :], var_eps[NTH[task] % NM][:, :], neghalf[:, :], ALU.pow).then_inc(rstd_done, 1)
                    elif kind == "norm" and t == 2:
                        layer, b = BLOCKS[k]
                        pool.wait_ge(norm_done, NTH[task] + 1)
                        gamma = rows_sb[:, GAMMA:GAMMA + 1, :].broadcast_to([128, QT, D])
                        beta = rows_sb[:, BETA:BETA + 1, :].broadcast_to([128, QT, D])
                        link(nc.gpsimd.tensor_tensor(z[:, :, :], z[:, :, :], gamma, ALU.mult))
                        link(nc.gpsimd.tensor_tensor(z[:, :, :], z[:, :, :], beta, ALU.add))
                        nc.gpsimd.tensor_tensor(res[:, b, :, :], res[:, b, :, :], z[:, :, :], ALU.add).then_inc(ffn0_added, 1)
                    elif kind == "add_bo":
                        layer, b = BLOCKS[k]
                        if NTH[task] == 0:
                            pool.wait_ge(small_in, 48)
                        pool.wait_ge(norm_done, NTH[("norm", k, 0)] + 1)
                        bo = rows_sb[:, (BO0, BO1)[layer]:(BO0, BO1)[layer] + 1, :].broadcast_to([128, QT, D])
                        nc.gpsimd.tensor_tensor(res[:, b, :, :], res[:, b, :, :], bo, ALU.add).then_inc(bo_added, 1)

        @block.scalar
        def _(act):
            act.dma_start(res[:, 0, :, :], x[0].rearrange("(t p) d -> p t d", p=128)).then_inc(x_in[0], 16)
            for half in range(FIRST, LAST + 1):
                step, odd = half // 2, half % 2
                if 0 <= step < STEPS:
                    layer, _b = BLOCKS[step // PER_BLOCK]
                    act.wait_ge(st_filled, half + 1)
                    if step >= NP and not odd:
                        act.wait_ge(pv_done, step - NP + 1)
                    nc.scalar.activation(probs[step % NP][:, 2 * odd:2 * odd + 2, :], st[half % NST][:, :, :], ACT.Exp,
                                         scale=SCALES[layer]).then_inc(exp_done, 1)
                if step > KT and step % KT == 1 and step // KT <= UNITS and not odd:
                    u = step // KT - 1
                    act.wait_ge(pv_done, KT * (u + 1))
                    if u >= NJ and u % NJ == 0:
                        act.wait_ge(filled, JOB[("out_t", u // NJ - 1, 1)] + 1)
                    nc.scalar.activation(o_raw[:, u % NJ, :], pv[:, 0:S], ACT.Copy).then_inc(pv_emptied, 1)
                for task in TASKS.get(half, []):
                    kind, k, t = task
                    if task in JOB:
                        bank = JOB[task] % 2
                        side, side16 = sides[bank], sides16[bank]
                    if kind in ("proj_k", "x_t", "proj_q", "proj_v", "heads_t", "xq_t", "spread_scale", "hid_t", "hq_t", "max_t"):
                        act.wait_ge(filled, JOB[task] + 1)
                    if kind == "proj_k":
                        layer, b = BLOCKS[k]
                        if NTH[task] >= 2:
                            act.wait_ge(k_split, 2 * (NTH[task] // 2))
                            act.wait_ge(k_written, 16 * (NTH[task] // 2))
                        elif layer == 1:
                            act.wait_ge(small_in, 48)
                        src, _rest, parts = k_split_aps(t)
                        for dst in (parts[0], src):
                            if layer == 0:
                                ins = nc.scalar.activation(dst, side[:, 0:S], ACT.Copy)
                            else:
                                ins = nc.scalar.activation(dst, side[:, 0:S], ACT.Identity, bias=cols_sb[:, 1:2])
                        ins.then_inc(emptied[bank], 1)
                    elif kind == "proj_q":
                        layer, b = BLOCKS[k]
                        if NTH[task]:
                            act.wait_ge(q_split, 2 * NTH[task])
                            act.wait_ge(q_written, 48 * NTH[task])
                        for dst in (q_parts[:, 0, :], q_f[:, :]):
                            if layer == 0:
                                ins = nc.scalar.activation(dst, side[:, 0:S], ACT.Copy)
                            else:
                                ins = nc.scalar.activation(dst, side[:, 0:S], ACT.Identity, bias=cols_sb[:, 0:1])
                        ins.then_inc(emptied[bank], 1)
                    elif kind == "proj_v":
                        layer, b = BLOCKS[k]
                        old = AT_BLOCK.get((layer, b - 2))
                        if old is not None:
                            act.wait_ge(pv_done, PER_BLOCK * (old + 1))
                        if old is None:
                            act.wait_ge(v_set[layer][b], 1)
                        nc.scalar.activation(vst[layer][b % 2][:, 2 * t:2 * t + 2, :, 0:DH],
                                             side[:, 0:S].rearrange("p (t h d) -> p t h d", t=2, h=H), ACT.Copy).then_inc(emptied[bank], 1)
                    elif kind == "x_t":
                        nc.scalar.activation(x_t[:, :], side[:, 0:S], ACT.Copy).then_inc(emptied[bank], 1)
                    elif kind == "heads_t":
                        nc.scalar.activation(o_t[:, :], side[:, 0:S], ACT.Copy).then_inc(emptied[bank], 1)
                    elif kind == "xq_t":
                        nc.scalar.activation(a_t[:, :], side16[:, 0:S], ACT.Copy).then_inc(emptied[bank], 1)
                    elif kind == "spread_scale":
                        nc.scalar.activation(back_rows[:, :], side[:, 0:S], ACT.Copy).then_inc(emptied[bank], 1)
                    elif kind == "hq_t":
                        nc.scalar.activation(h_t[:, t, :, :].rearrange("p c n -> p (c n)"), side16[:, 0:HID], ACT.Copy).then_inc(emptied[bank], 1)
                    elif kind == "max_t":
                        if k >= 2:
                            act.wait_ge(max_placed[k % 2], 32 * (k // 2))
                        nc.scalar.activation(max_rows[k % 2][:, :], side16[0:2 * HG, 0:S], ACT.Copy).then_inc(emptied[bank], 1)
                    elif kind == "conv":
                        wait_emptied(act, ("up", k, t))
                        if NTH[task] >= 2:
                            act.wait_ge(filled, JOB[[q for q in JOB if q[0] == "hid_t"][2 * (NTH[task] // 2) - 1]] + 1)
                        if NTH[task] == 0:
                            act.wait_ge(small_in, 48)
                        for c in (2 * t, 2 * t + 1):
                            nc.scalar.activation(y[:, c, :], hid[:, c, 1:S + 1], ACT.Identity, bias=conv_sb[:, c, 3:4],
                                                 scale=conv_sb[:, c, 1:2]).then_inc(tapped, 1)
                    elif kind == "silu":
                        act.wait_ge(conved, NTH[task] + 1)
                        nc.scalar.activation(tanh_y[:, 2 * t:2 * t + 2, :], y[:, 2 * t:2 * t + 2, :], ACT.Tanh, scale=0.5).then_inc(tanhed, 1)
                    elif kind == "hid_t":
                        if NTH[task] >= QT:
                            act.wait_ge(h_quant, NTH[task] - QT + 1)
                        nc.scalar.activation(h_tmp[:, t, :], side[:, :], ACT.Copy).then_inc(emptied[bank], 1)

        @block.vector
        def _(dve):
            chain = [0]

            def link(ins):
                chain[0] += 1
                ins.then_inc(v_step, 1)
                dve.wait_ge(v_step, chain[0])

            link(nc.vector.memset(vst[0][0][:, :, :, :].rearrange("p t h d -> p (t h d)"), 0.0))
            nc.vector.memset(vst[0][0][:, :, :, DH:DH + 1], 1.0).then_inc(v_set[0][0], 1)
            for half in range(FIRST, LAST + 1):
                count = half + 8 * LEAD
                u, n = count // 8, count % 8
                if 0 <= u < UNITS:
                    layer, _b = BLOCKS[u // NJ]
                    if u >= 2 and n == 0:
                        dve.wait_ge(max_split, u - 1)
                    if layer == 1 and u // NJ == AT_BLOCK[(1, 0)] and n == 0:
                        dve.wait_ge(mask_set, 1)
                    dve.wait_ge(sm_filled, count + 1)
                    m_out = row_max[u % 2][:, n // HG, n % HG:n % HG + 1]
                    if layer == 0:
                        nc.vector.tensor_reduce(m_out, sm[count % 2][:, :], X, ALU.max).then_inc(max_taken, 1)
                    else:
                        dve.wait_ge(max_taken, count - 1)
                        nc.vector.tensor_tensor_reduce(masked[:, n % 2, :], sm[count % 2][:, :], mask_max[:, n // HG, :],
                                                       1.0, MASK_EXP, ALU.add, ALU.max, m_out).then_inc(max_taken, 1)
                for task in TASKS.get(half, []):
                    kind, k, t = task
                    if task in JOB:
                        bank = JOB[task] % 2
                        side = sides[bank]
                    if kind == "stats":
                        layer, b = BLOCKS[k]
                        src = z if (layer == 0 and t == 2) else res[:, b, :, :]
                        if layer == 0 and t == 2:
                            dve.wait_ge(norm_done, NTH[("norm", k, 1)] + 1)
                        else:
                            res_writers(dve, k, t)
                        m = NTH[task] % NM
                        if NTH[task] >= NM:
                            dve.wait_ge(norm_done, NTH[task] - NM + 1)
                        for i in range(QT):
                            ins = nc.vector.bn_stats(bn[m][:, i, :], src[:, i, :])
                        link(ins)
                        for i in range(QT):
                            ins = nc.vector.bn_aggr(moments[m][:, i, :], bn[m][:, i, :])
                        ins.then_inc(stats_done, 1)
                    elif kind == "norm":
                        layer, b = BLOCKS[k]
                        dst, m = norm_target(k, t), NTH[task] % NM
                        src = z if (layer == 0 and t == 2) else res[:, b, :, :]
                        dve.wait_ge(rstd_done, NTH[task] + 1)
                        if t == 0:
                            before = [q for q in JOB if q[0] == "x_t" and BLOCKS[q[1]][0] == layer and NTH[q] < NTH[("x_t", k, 0)]]
                            if before:
                                dve.wait_ge(filled, JOB[before[-1]] + 1)
                        if layer == 0 and t == 1 and b:
                            dve.wait_ge(ffn0_added, b)
                        for i in range(QT):
                            ins = nc.vector.tensor_scalar(dst[:, i, :], src[:, i, :], moments[m][:, i, 0:1], rstd[m][:, i:i + 1],
                                                          ALU.subtract, ALU.mult)
                        ins.then_inc(norm_done, 1)
                    elif kind == "out_t":
                        dve.wait_ge(filled, JOB[task] + 1)
                        if NTH[task] >= QT and t == 0:
                            dve.wait_ge(filled, JOB[[q for q in JOB if q[0] == "heads_t"][NTH[task] // QT - 1]] + 1)
                        o_nat = side[:, :].rearrange("p (j g c) -> p j g c", j=NJ, g=HG)
                        link(nc.vector.reciprocal(inv_den[:, t, :, :], o_nat[:, :, :, DH]))
                        nc.vector.tensor_tensor(o_heads[:, t, :, :],
                                                side[:, :].rearrange("p (h c) -> p h c", h=H)[:, :, 0:DH],
                                                inv_den[:, t, :, :].rearrange("p j g -> p (j g)").unsqueeze(2).broadcast_to([128, H, DH]),
                                                ALU.mult).then_inc(emptied[bank], 1)
                    elif kind == "proj_o":
                        layer, b = BLOCKS[k]
                        dve.wait_ge(filled, JOB[task] + 1)
                        dve.wait_ge(bo_added, NTH[("add_bo", k, 0)] + 1)
                        flat = res[:, b, :, :].rearrange("p t d -> p (t d)")
                        nc.vector.tensor_tensor(flat, side[:, 0:S], flat, ALU.add).then_inc(emptied[bank], 1)
                    elif kind == "weight_mean":
                        dve.wait_ge(ffn_in, 32)
                        nc.vector.tensor_reduce(w_sum[:, 0:1], w1_sb[:, :], X, ALU.add, apply_absolute_value=True).then_inc(w_summed, 1)
                        nc.vector.tensor_reduce(w_sum[:, 1:2], w2_sb[:, :, :].rearrange("p c n -> p (c n)"), X, ALU.add,
                                                apply_absolute_value=True).then_inc(w_summed, 1)
                        dve.wait_ge(filled, JOB[task] + 1)
                        nc.vector.tensor_scalar(w_mean[:, :], side[:, 0:2], 1.0 / (D * HID), EPS, ALU.mult, ALU.max).then_inc(emptied[bank], 1)
                        wait_emptied(dve, task)
                        nc.vector.reciprocal(w_inv[:, :], w_mean[:, :]).then_inc(w_mean_set, 1)
                    elif kind == "mask":
                        dve.wait_ge(mask_in, 32)
                        nc.vector.tensor_scalar(mask_max[:, :, :], mask_i[:, :, :], 0.0, MASK_MAX, ALU.is_equal, ALU.mult).then_inc(mask_set, 1)
                        for i in range(2):
                            nc.vector.tensor_scalar(mask_exp[:, :, i, :], maskT_i[:, :, :], 0.0, MASK_EXP, ALU.is_equal, ALU.mult).then_inc(mask_set, 1)
                    elif kind == "quant_w":
                        dve.wait_ge(w_mean_set, 1)
                        for i, (w, q) in enumerate(((w1_sb[:, :], w1_q[:, :]),
                                                    (w2_sb[:, :, :].rearrange("p c n -> p (c n)"),
                                                     w2_q[:, :, :].rearrange("p c n -> p (c n)")))):
                            link(nc.vector.tensor_scalar(w_tmp, w, w_inv[:, i:i + 1], ROUND, ALU.mult, ALU.add))
                            link(nc.vector.tensor_scalar(w_tmp, w_tmp, ROUND, 1.0, ALU.subtract, ALU.min))
                            ins = nc.vector.tensor_scalar(q, w_tmp, -1.0, None, ALU.max)
                            if i == 0:
                                link(ins)
                        ins.then_inc(w_quant, 1)
                    elif kind == "split_k" and k == 0:
                        wait_emptied(dve, ("proj_k", k, t))
                        src, rest, parts = k_split_aps(t)
                        link(nc.vector.tensor_tensor(rest, src, parts[0], ALU.subtract))
                        link(nc.vector.tensor_copy(parts[1], rest))
                        nc.vector.tensor_tensor(parts[2], rest, parts[1], ALU.subtract).then_inc(k_split, 1)
                    elif kind == "split_q" and k == 0:
                        wait_emptied(dve, ("proj_q", k, 0))
                        n = 2 * NTH[task]
                        src, rest, parts = q_split_aps()
                        link(nc.vector.tensor_tensor(rest, src, parts[0], ALU.subtract))
                        nc.vector.tensor_copy(parts[1], rest).then_inc(q_split, 1)
                        dve.wait_ge(q_split, n + 1)
                        nc.vector.tensor_tensor(parts[2], rest, parts[1], ALU.subtract).then_inc(q_split, 1)
                    elif kind == "quant_x":
                        dve.wait_ge(norm_done, NTH[("norm", k, 1)] + 1)
                        if NTH[task]:
                            dve.wait_ge(filled, JOB[[q for q in JOB if q[0] == "spread_scale"][NTH[task] - 1]] + 1)
                        link(nc.vector.tensor_reduce(amax[:, :], xf[:, :, :], X, ALU.max, apply_absolute_value=True))
                        link(nc.vector.tensor_scalar(amax[:, :], amax[:, :], EPS, None, ALU.max))
                        link(nc.vector.reciprocal(a_inv[:, :], amax[:, :]))
                        nc.vector.tensor_scalar(a_back[:, :], amax[:, :], w_mean[:, 0:1], 1.0 / 127.0, ALU.mult, ALU.mult)
                        link(nc.vector.tensor_scalar(a_scale[:, :], a_inv[:, :], 127.0, None, ALU.mult))
                        for i in range(QT):
                            ins = nc.vector.tensor_scalar(a_tmp[:, i, :], xf[:, i, :], a_scale[:, i:i + 1], ROUND, ALU.mult, ALU.add)
                        link(ins)
                        nc.vector.tensor_scalar(a_q[:, :, :], a_tmp[:, :, :], ROUND, None, ALU.subtract).then_inc(x_quant, 1)
                        for i in range(QT):
                            ins = nc.vector.tensor_scalar(back_diag[:, i, :], id32[:, :], a_back[:, i:i + 1], None, ALU.mult)
                        ins.then_inc(x_quant, 1)
                    elif kind == "up":
                        dve.wait_ge(filled, JOB[task] + 1)
                        if t == 0:
                            wait_emptied(dve, ("spread_scale", k, 0))
                            if NTH[task] == 0:
                                dve.wait_ge(hid_set, 1)
                            else:
                                dve.wait_ge(tapped, CH * (NTH[task] // 2))
                        nc.vector.tensor_tensor(hid[:, 2 * t:2 * t + 2, 1:S + 1],
                                                side[:, :].rearrange("p (c s) -> p c s", c=2),
                                                back_rows[:, :].unsqueeze(1).broadcast_to([128, 2, S]), ALU.mult).then_inc(emptied[bank], 1)
                    elif kind == "conv":
                        for c in (2 * t, 2 * t + 1):
                            dve.wait_ge(tapped, CH * (NTH[task] // 2) + c + 1)
                            link(nc.vector.scalar_tensor_tensor(y[:, c, :], hid[:, c, 0:S], conv_sb[:, c, 0:1], y[:, c, :],
                                                                ALU.mult, ALU.add))
                            ins = nc.vector.scalar_tensor_tensor(y[:, c, :], hid[:, c, 2:S + 2], conv_sb[:, c, 2:3], y[:, c, :],
                                                                 ALU.mult, ALU.add)
                        ins.then_inc(conved, 1)
                    elif kind == "silu":
                        dve.wait_ge(tanhed, NTH[task] + 1)
                        flat = [a[:, 2 * t:2 * t + 2, :].rearrange("p c s -> p (c s)") for a in (tanh_y, y)]
                        nc.vector.scalar_tensor_tensor(flat[1], flat[0], 1.0, flat[1], ALU.add, ALU.mult).then_inc(silued, 1)
                    elif kind == "quant_h":
                        wait_emptied(dve, ("hid_t", k, t))
                        if NTH[task] >= QT:
                            dve.wait_ge(filled, JOB[[q for q in JOB if q[0] == "hq_t"][NTH[task] - QT]] + 1)
                        m, inv, row = h_max[:, t:t + 1], h_inv[:, t:t + 1], h_tmp[:, t, :]
                        link(nc.vector.tensor_reduce(m, row, X, ALU.max, apply_absolute_value=True))
                        link(nc.vector.tensor_scalar(m, m, 2 * EPS, None, ALU.max))
                        link(nc.vector.reciprocal(inv, m))
                        nc.vector.tensor_scalar(h_back[:, t:t + 1], m, w_mean[:, 1:2], 0.5 / 127.0, ALU.mult, ALU.mult)
                        link(nc.vector.tensor_scalar(h_scale[:, t:t + 1], inv, 127.0, None, ALU.mult))
                        link(nc.vector.tensor_scalar(row, row, h_scale[:, t:t + 1], ROUND, ALU.mult, ALU.add))
                        nc.vector.tensor_scalar(h_q[:, t, :], row, ROUND, None, ALU.subtract).then_inc(h_quant, 1)
                    elif kind == "down":
                        _, b = BLOCKS[k]
                        dve.wait_ge(filled, JOB[task] + 1)
                        if NTH[task]:
                            dve.wait_ge(stored, 16 * NTH[task])
                        for i in range(QT):
                            ins = nc.vector.scalar_tensor_tensor(y_out[:, i, :], side[:, 128 * i:128 * i + 128], h_back[:, i:i + 1],
                                                                 res[:, b, i, :], ALU.mult, ALU.add)
                        ins.then_inc(emptied[bank], 1)

        @block.tensor
        def _(pe):
            def scores_t(n):
                step, odd = n // 2, n % 2
                k, j, kt = step // PER_BLOCK, step // KT % NJ, step % KT
                layer, b = BLOCKS[k]
                ks, qs, u = kst[layer][b % 2], qst[layer][b % 2], step // KT
                if kt == 0 and not odd:
                    pe.wait_ge(max_placed[u % 2], 32 * (u // 2 + 1))
                if n >= NST:
                    pe.wait_ge(exp_done, n - NST + 1)
                if layer == 1:
                    if n == 2 * PER_BLOCK * AT_BLOCK[(1, 0)]:
                        pe.wait_ge(mask_set, 3)
                    nc.tensor.matmul(st[n % NST][:, :, :], id16[:, :], mask_exp[:, kt, :, :], start=True, stop=False)
                for g in range(2):
                    h = HG * j + 2 * odd + g
                    ins = nc.tensor.matmul(st[n % NST][:, g, :], ks[:, h % 8, 128 * kt:128 * kt + 128], qs[:, h, :],
                                           start=layer == 0, stop=layer == 0 or g == 1)
                ins.then_inc(st_filled, 1)

            def scores(u, n):
                k, j, t, g = u // NJ, u % NJ, n // HG, n % HG
                layer, b = BLOCKS[k]
                count = 8 * u + n
                if j == 0 and n == 0:
                    pe.wait_ge(kq_read[k], 160)
                    if b < 2:
                        pe.wait_ge(k_ones[2 * layer + b], 32)
                        pe.wait_ge(q_zeros, 4 * layer + 2 * b + 2)
                if count >= 2:
                    pe.wait_ge(max_taken, count - 1)
                h = HG * j + g
                nc.tensor.matmul(sm[count % 2][:, :], qst[layer][b % 2][:, h, 128 * t:128 * t + 128],
                                 kst[layer][b % 2][:, h % 8, :], start=True, stop=True).then_inc(sm_filled, 1)

            def weighted(step):
                k, j, kt = step // PER_BLOCK, step // KT % NJ, step % KT
                layer, b = BLOCKS[k]
                if step % PER_BLOCK == 0:
                    wait_emptied(pe, ("proj_v", k, 0))
                    wait_emptied(pe, ("proj_v", k, 1))
                if kt == 0 and step:
                    pe.wait_ge(pv_emptied, step // KT)
                pe.wait_ge(exp_done, 2 * step + 2)
                for g in range(HG):
                    ins = nc.tensor.matmul(pv[32 * g:32 * g + 32, 0:S], vst[layer][b % 2][:, kt, HG * j + g, :],
                                           probs[step % NP][:, g, :], start=kt == 0, stop=kt == KT - 1)
                ins.then_inc(pv_done, 1)

            def job(task):
                kind, k, t = task
                n = JOB[task]
                side, side16 = sides[n % 2], sides16[n % 2]
                if n >= 2:
                    pe.wait_ge(emptied[n % 2], n // 2)
                if kind == "proj_k":
                    layer, b = BLOCKS[k]
                    if k == 0 and t == 0:
                        pe.wait_ge(proj_in[0], 16)
                    elif layer == 1 and b == 0 and t == 0:
                        pe.wait_ge(proj_in[1], 16)
                    pe.wait_ge(ctx_in[min(b, 1)], 16)
                    ins = nc.tensor.matmul(side[:, 0:S], proj[:, 4 * layer + 1, :], ctx_sb[:, b, S * t:S * t + S], start=True, stop=True)
                elif kind == "proj_v":
                    layer, b = BLOCKS[k]
                    if k == 0 and t == 0:
                        pe.wait_ge(proj_in[1], 16)
                    if layer == 1 and b == 0 and t == 0:
                        pe.wait_ge(small_in, 48)
                    for i in range(2):
                        sl, kt = side[:, 128 * i:128 * i + 128], 2 * t + i
                        ins = nc.tensor.matmul(sl, ctx_sb[:, b, 128 * kt:128 * kt + 128], proj[:, 4 * layer + 2, :],
                                               start=True, stop=layer == 0)
                        if layer == 1:
                            ins = nc.tensor.matmul(sl, ones[0:1, :], rows_sb[0:1, BV1, :], start=False, stop=True)
                elif kind == "x_t":
                    layer, b = BLOCKS[k]
                    pe.wait_ge(norm_done, NTH[("norm", k, 0)] + 1)
                    if NTH[task] == 0:
                        pe.wait_ge(id_set, 1)
                    for i in range(QT):
                        ins = nc.tensor.transpose(side[:, 128 * i:128 * i + 128], xq[layer][:, i, :], id32[:, :])
                elif kind == "proj_q":
                    layer, b = BLOCKS[k]
                    wait_emptied(pe, ("x_t", k, 0))
                    ins = nc.tensor.matmul(side[:, 0:S], proj[:, 4 * layer, :], x_t[:, :], start=True, stop=True)
                elif kind == "max_t":
                    pe.wait_ge(max_split, k + 1)
                    for i in range(QT):
                        ins = nc.tensor.transpose(side16[0:2 * HG, 128 * i:128 * i + 128],
                                                  max_parts[k % 2][:, i, :, :].rearrange("p a g -> p (a g)"), id16[:, :])
                elif kind == "out_t":
                    pe.wait_ge(pv_emptied, NJ * (k + 1))
                    for j in range(NJ):
                        ins = nc.tensor.transpose(side[:, 128 * j:128 * j + 128], o_raw[:, j, 128 * t:128 * t + 128], id32[:, :])
                elif kind == "heads_t":
                    wait_emptied(pe, ("out_t", k, 1))
                    for i in range(QT):
                        ins = nc.tensor.transpose(side[:, 128 * i:128 * i + 128],
                                                  o_heads[:, i, :, :].rearrange("p h d -> p (h d)"), id32[:, :])
                elif kind == "proj_o":
                    layer, b = BLOCKS[k]
                    wait_emptied(pe, ("heads_t", k, 0))
                    for i in range(QT):
                        ins = nc.tensor.matmul(side[:, 128 * i:128 * i + 128], o_t[:, 128 * i:128 * i + 128],
                                               proj[:, 4 * layer + 3, :], start=True, stop=True)
                elif kind == "weight_mean":
                    pe.wait_ge(w_summed, 2)
                    pe.wait_ge(ones_set, 1)
                    ins = nc.tensor.matmul(side[:, 0:2], ones[:, :], w_sum[:, :], start=True, stop=True)
                elif kind == "xq_t":
                    pe.wait_ge(x_quant, 2 * NTH[task] + 1)
                    for i in range(QT):
                        ins = nc.tensor.transpose(side16[:, 128 * i:128 * i + 128], a_q[:, i, :], id16[:, :])
                elif kind == "spread_scale":
                    pe.wait_ge(x_quant, 2 * NTH[task] + 2)
                    ins = nc.tensor.matmul(side[:, 0:S], ones[:, :], back_diag[:, :, :].rearrange("p t s -> p (t s)"),
                                           start=True, stop=True)
                elif kind == "up":
                    if t == 0:
                        wait_emptied(pe, ("xq_t", k, 0))
                        if NTH[task] == 0:
                            pe.wait_ge(w_quant, 1)
                    for i in range(2):
                        c = 2 * t + i
                        ins = nc.tensor.matmul(side[:, S * i:S * i + S], w1_q[:, 128 * c:128 * c + 128], a_t[:, :],
                                               start=True, stop=True)
                elif kind == "hid_t":
                    pe.wait_ge(silued, NTH[("silu", k, 1)] + 1)
                    for c in range(CH):
                        ins = nc.tensor.transpose(side[:, 128 * c:128 * c + 128], y[:, c, 128 * t:128 * t + 128], id32[:, :])
                elif kind == "hq_t":
                    pe.wait_ge(h_quant, NTH[("quant_h", k, t)] + 1)
                    for c in range(CH):
                        ins = nc.tensor.transpose(side16[:, 128 * c:128 * c + 128], h_q[:, t, 128 * c:128 * c + 128], id16[:, :])
                elif kind == "down":
                    wait_emptied(pe, ("hq_t", k, 1))
                    for i in range(QT):
                        for c in range(CH):
                            ins = nc.tensor.matmul(side[:, 128 * i:128 * i + 128], h_t[:, i, c, :], w2_q[:, c, :],
                                                   start=c == 0, stop=c == CH - 1)
                ins.then_inc(filled, 1)

            for half in range(FIRST, LAST + 1):
                if 0 <= half + 2 < 2 * STEPS:
                    scores_t(half + 2)
                count = half + 8 * LEAD
                if 0 <= count < 8 * UNITS:
                    scores(count // 8, count % 8)
                for task in TASKS.get(half, []):
                    if task in JOB:
                        job(task)
                if half % 2 == 0 and 0 <= half // 2 - 1 < STEPS:
                    weighted(half // 2 - 1)


def kernel(**inputs):
    import numpy as np
    import concourse.bacc as bacc
    from concourse.bass_utils import run_bass_kernel_spmd

    a = {name: np.asarray(value) for name, value in inputs.items()}
    by_dim = np.arange(D).reshape(H, DH).T.reshape(-1)
    arrays = {
        "x": a["x"],
        "ctxT": a["ctx_1024"].transpose(0, 2, 1),
        "projT": np.stack([
            a["L0_xattn_Wq"][by_dim].T, a["L0_xattn_Wk"][by_dim].T, a["L0_xattn_Wv"].T, a["L0_xattn_Wo"].T,
            a["L1_xattn_w_q"][by_dim].T, a["L1_xattn_w_k"][by_dim].T, a["L1_xattn_w_v"].T, a["L1_xattn_w_o"].T], axis=1),
        "rows": np.stack([a["L0_xattn_bo"], a["L0_ffn_ln_g"], a["L0_ffn_ln_b"], a["L1_xattn_b_o"], a["L1_xattn_b_v"]]),
        "cols": np.stack([a["L1_xattn_b_q"][by_dim], a["L1_xattn_b_k"][by_dim]], axis=1),
        "mask": a["mask_1x1xSxS2_ik0"][0, 0],
        "maskT": a["mask_1x1xSxS2_ik0"][0, 0].T,
        "w1T": a["L1_ffn_w1"].T,
        "conv": np.concatenate([a["L1_ffn_conv_w"][:, 0, :], a["L1_ffn_conv_b"][:, None]], axis=1),
        "w2T": a["L1_ffn_w2"].T,
    }
    arrays = {name: np.ascontiguousarray(value) for name, value in arrays.items()}
    nc = bacc.Bacc("TRN2", target_bir_lowering=False, num_devices=1)
    aps = [nc.dram_tensor(name, value.shape, mybir.dt.from_np(value.dtype), kind="ExternalInput").ap()
           for name, value in arrays.items()]
    out = nc.dram_tensor("out", (B, S, D), mybir.dt.float32, kind="ExternalOutput").ap()
    build(nc, *aps, out)
    result = run_bass_kernel_spmd(nc, [arrays], core_ids=[0])
    return result.results[0]["out"]
```

```python
import concourse.bass as bass
from concourse import mybir
from contextlib import ExitStack

B, S, D = 4, 256, 128
SK = 512
H, DH = 16, 8
HID = 512
QT, KT, CH = S // 128, SK // 128, HID // 128
HG = 4
NJ = H // HG
EPS = 1e-5
SCALES = (D ** -0.5, DH ** -0.5)
ROUND = 12582912.0
MASK_MAX, MASK_EXP = -1e30, -3e38

BLOCKS = [(0, 0), (0, 1), (0, 2), (1, 0), (0, 3), (1, 1), (1, 2), (1, 3)]
NB = len(BLOCKS)
AT_BLOCK = {lb: k for k, lb in enumerate(BLOCKS)}
UNITS = NB * NJ
STEPS = UNITS * KT
LEAD = 24
PER_BLOCK = NJ * KT
NST = 3
NM = 3
NP = 4


def schedule():
    at = {}

    def add(step, *task):
        at.setdefault(round(2 * step), []).append(task)

    add(-26, "clear", 0, 0)
    add(-26, "clear", 1, 0)
    for k, (layer, b) in enumerate(BLOCKS):
        s = PER_BLOCK * k - (26 if k == 1 else 28)
        old = AT_BLOCK.get((layer, b - 2))
        free = PER_BLOCK * (old + 1) if old is not None else -99
        if layer == 0:
            add(s, "stats", k, 0)
        add(s + 1, "proj_k", k, 0)
        add(s + 1, "split_k", k, 0)
        if layer == 0:
            add(s + 1, "norm", k, 0)
        add(s + 2, "proj_k", k, 1)
        add(s + 2, "split_k", k, 1)
        if layer == 0:
            add(s + 2.5, "x_t", k, 0)
        add(s + 3, "write_k", k, 0)
        if layer == 0:
            add(s + 3.5, "proj_q", k, 0)
            add(s + 3.5, "split_q", k, 0)
            add(s + 4, "write_q", k, 0)
            add(s + 4, "add_bo", k, 0)
        add(max(s + 5, free + 1), "proj_v", k, 0)
        add(max(s + 6, free + 2), "proj_v", k, 1)
        add(max(s + 6, free), "read_k", k, 0)
        if layer == 0:
            add(max(s + 7, free), "read_q", k, 0)
        e = PER_BLOCK * (k + 1)
        add(e + 1, "out_t", k, 0)
        add(e + 1.5, "out_t", k, 1)
        add(e + 3, "heads_t", k, 0)
        add(e + 4, "proj_o", k, 0)
        add(e + 5, "stats", k, 1)
        add(e + 6, "norm", k, 1)
        if layer == 0:
            k1 = AT_BLOCK[(1, b)]
            old = AT_BLOCK.get((1, b - 2))
            free = PER_BLOCK * (old + 1) if old is not None else -99
            add(e + 8, "stats", k, 2)
            add(e + 9, "norm", k, 2)
            add(e + 11, "stats", k1, 0)
            add(e + 12, "norm", k1, 0)
            add(e + 13, "x_t", k1, 0)
            add(e + 14, "proj_q", k1, 0)
            add(e + 14, "split_q", k1, 0)
            add(e + 14, "add_bo", k1, 0)
            add(e + 15, "write_q", k1, 0)
            add(max(e + 17, free), "read_q", k1, 0)
        else:
            add(e + 7, "max_x", k, 0)
            add(e + 7, "back_x", k, 0)
            add(e + 7.5, "round_x", k, 0)
            add(e + 8, "spread_scale", k, 0)
            add(e + 8.5, "xq_t", k, 0)
            add(e + 9.5, "up", k, 0)
            add(e + 10, "tap", k, 0)
            add(e + 10, "up", k, 1)
            add(e + 10.5, "tap", k, 1)
            add(e + 10.5, "conv", k, 0)
            add(e + 11, "conv", k, 1)
            add(e + 11.5, "conv", k, 2)
            add(e + 12, "conv", k, 3)
            add(e + 12, "silu", k, 0)
            add(e + 13, "silu", k, 1)
            late = k == NB - 2
            add(e + (18 if late else 14), "hid_t", k, 0)
            add(e + (18.5 if late else 14.5), "hid_t", k, 1)
            add(e + (18.5 if late else 14.5), "max_h", k, 0)
            add(e + (19 if late else 15), "max_h", k, 1)
            f = e + (21.5 if late else 15.5)
            add(f, "scale_h", k, 0)
            add(f, "round_h", k, 0)
            add(f + 0.5, "round_h", k, 1)
            add(f + 1, "hq_t", k, 0)
            add(f + 1.5, "hq_t", k, 1)
            last = e + (29.5 if late else 18)
            add(last, "down", k, 0)
            add(last + 0.5, "store", k, 0)
    for u in range(UNITS):
        add(KT * (u + 1) - LEAD / 2, "split_max", u, 0)
        add(KT * (u + 1) - LEAD / 2 + 2.5, "max_t", u, 0)
    add(-20.5, "load_second", 0, 0)
    add(-20.5, "load_rest", 0, 0)
    add(-20, "mask", 0, 0)
    add(-19, "weight_mean", 0, 0)
    add(-18, "quant_w", 0, 0)
    return at


TASKS = schedule()
FIRST, LAST = min(TASKS), max(max(TASKS), 2 * STEPS)
ORDER = [task for half in range(FIRST, LAST + 1) for task in TASKS.get(half, [])]
JOBS = ("proj_k", "x_t", "proj_q", "proj_v", "out_t", "heads_t", "proj_o", "xq_t", "spread_scale", "up",
        "hid_t", "hq_t", "down", "max_t", "weight_mean")
JOB = {task: n for n, task in enumerate(t for t in ORDER if t[0] in JOBS)}
NTH = {}
for _task in ORDER:
    NTH[_task] = sum(1 for t in NTH if t[0] == _task[0])


def build(nc, x, ctxT, projT, rows, cols, mask, maskT, w1T, conv, w2T, out):
    f32, bf16, i32 = mybir.dt.float32, mybir.dt.bfloat16, mybir.dt.int32
    ALU = mybir.AluOpType
    ACT = mybir.ActivationFunctionType
    X = mybir.AxisListType.X
    BO0, GAMMA, BETA, BO1, BV1 = range(5)

    k_scratch = nc.dram_tensor("k_scratch", [NB, 6, 128, SK], bf16).ap()
    q_scratch = nc.dram_tensor("q_scratch", [NB, 6, 128, S], bf16).ap()

    es = ExitStack()
    with es:
        def sb(name, shape, dt=f32):
            return es.enter_context(nc.sbuf_tensor(name, shape, dt))

        def sem(name):
            return es.enter_context(nc.semaphore(name))

        res = sb("res", [128, B, QT, D])
        ctx_sb = sb("ctx_sb", [128, B, SK])
        proj = sb("proj", [128, 8, D])
        rows_sb = sb("rows_sb", [128, 5, D])
        cols_sb = sb("cols_sb", [128, 2])
        mask_i = sb("mask_i", [128, QT, SK], i32)
        maskT_i = sb("maskT_i", [128, KT, S], i32)
        w1_sb = sb("w1_sb", [128, HID])
        w2_sb = sb("w2_sb", [128, CH, D])
        conv_sb = sb("conv_sb", [128, CH, 4])
        id32 = sb("id32", [128, 128])
        id16 = sb("id16", [128, 128], bf16)
        ones = sb("ones", [128, 128])
        minus16 = sb("minus16", [128, 512], bf16)
        zeros16 = sb("zeros16", [128, 256], bf16)
        neghalf = sb("neghalf", [128, QT])
        round_bias = sb("round_bias", [128, 2])
        kst = [[sb(f"kst{l}{i}", [128, H // 2, SK], bf16) for i in range(2)] for l in range(2)]
        qst = [[sb(f"qst{l}{i}", [128, H, S], bf16) for i in range(2)] for l in range(2)]
        vst = [[sb(f"vst{l}{i}", [128, KT, H, 32]) for i in range(2)] for l in range(2)]
        mask_max = sb("mask_max", [128, QT, SK])
        mask_exp = sb("mask_exp", [128, KT, 2, S], bf16)
        masked = sb("masked", [128, 2, SK], bf16)
        k_f = sb("k_f", [128, SK])
        k_rest = sb("k_rest", [128, SK])
        k_parts = sb("k_parts", [128, 3, SK], bf16)
        q_f = sb("q_f", [128, S])
        q_rest = sb("q_rest", [128, S])
        q_parts = sb("q_parts", [128, 3, S], bf16)
        row_max = [sb(f"row_max{i}", [128, QT, HG]) for i in range(2)]
        max_parts = [sb(f"max_parts{i}", [128, QT, 2, HG], bf16) for i in range(2)]
        max_rows = [sb(f"max_rows{i}", [2 * HG, S], bf16) for i in range(2)]
        probs = [sb(f"probs{i}", [128, HG, S]) for i in range(NP)]
        o_raw = sb("o_raw", [128, NJ, S])
        inv_den = sb("inv_den", [128, QT, NJ, HG])
        o_heads = sb("o_heads", [128, QT, H, DH])
        o_t = sb("o_t", [128, S])
        bn = [sb(f"bn{i}", [128, QT, 6]) for i in range(NM)]
        moments = [sb(f"moments{i}", [128, QT, 2]) for i in range(NM)]
        var_eps = [sb(f"var_eps{i}", [128, QT]) for i in range(NM)]
        rstd = [sb(f"rstd{i}", [128, QT]) for i in range(NM)]
        xq = [sb(f"xq{l}", [128, QT, D]) for l in range(2)]
        z = sb("z", [128, QT, D])
        xf = sb("xf", [128, QT, D])
        x_t = sb("x_t", [128, S])
        w_sum = sb("w_sum", [128, 2])
        w_mean = sb("w_mean", [128, 2])
        w_inv = sb("w_inv", [128, 2])
        w1_q = sb("w1_q", [128, HID], bf16)
        w2_q = sb("w2_q", [128, CH, D], bf16)
        amax = sb("amax", [128, QT])
        a_scale = sb("a_scale", [128, QT])
        a_back = sb("a_back", [128, QT])
        a_tmp = sb("a_tmp", [128, QT, D])
        a_q = sb("a_q", [128, QT, D], bf16)
        back_diag = sb("back_diag", [128, QT, 128])
        a_t = sb("a_t", [128, S], bf16)
        back_rows = sb("back_rows", [128, S])
        hid = sb("hid", [128, CH, S + 2])
        y = sb("y", [128, CH, S])
        w_tmp = y[:, 0:2, :].rearrange("p c s -> p (c s)")
        tanh_y = sb("tanh_y", [128, CH, S])
        h_max = sb("h_max", [128, QT])
        h_scale = sb("h_scale", [128, QT])
        h_back = sb("h_back", [128, QT])
        h_tmp = sb("h_tmp", [128, QT, HID])
        h_q = sb("h_q", [128, QT, HID], bf16)
        h_t = sb("h_t", [128, QT, CH, 128], bf16)
        y_out = sb("y_out", [128, QT, D])

        st = [es.enter_context(nc.psum_tensor(f"st{i}", [128, 2, S], f32)) for i in range(NST)]
        sm = [es.enter_context(nc.psum_tensor(f"sm{i}", [128, SK], f32)) for i in range(2)]
        pv = es.enter_context(nc.psum_tensor("pv", [128, S], f32))
        sides = [es.enter_context(nc.psum_tensor(f"side{i}", [128, 512], f32)) for i in range(2)]
        sides16 = [a[:, :].bitcast(bf16) for a in sides]

        x_in = [sem(f"x_in{i}") for i in range(3)]
        ctx_in = [sem(f"ctx_in{i}") for i in range(3)]
        proj_in = [sem(f"proj_in{i}") for i in range(2)]
        small_in = sem("small_in")
        mask_in = sem("mask_in")
        ffn_in = sem("ffn_in")
        k_written, q_written = sem("k_written"), sem("q_written")
        kq_read = [sem(f"kq_read{k}") for k in range(NB)]
        max_placed = [sem(f"max_placed{i}") for i in range(2)]
        stored = sem("stored")
        id_set, ones_set, minus16_set, hid_set = (
            sem(n) for n in ("id_set", "ones_set", "minus16_set", "hid_set"))
        k_ones = [sem(f"k_ones{i}") for i in range(4)]
        q_zeros, round_set = sem("q_zeros"), sem("round_set")
        v_set = [[sem(f"v_set{l}{i}") for i in range(2)] for l in range(2)]
        sm_filled, max_taken = sem("sm_filled"), sem("max_taken")
        st_filled, exp_done, pv_done, pv_emptied = (sem(n) for n in ("st_filled", "exp_done", "pv_done", "pv_emptied"))
        max_split = sem("max_split")
        filled = sem("filled")
        emptied = [sem(f"emptied{i}") for i in range(2)]

        def wait_emptied(eng, task):
            eng.wait_ge(emptied[JOB[task] % 2], JOB[task] // 2 + 1)

        k_split, q_split = sem("k_split"), sem("q_split")
        stats_done, rstd_done, norm_done = sem("stats_done"), sem("rstd_done"), sem("norm_done")
        ffn0_added, bo_added = sem("ffn0_added"), sem("bo_added")
        mask_set = sem("mask_set")
        w_summed, w_mean_set, w_quant = sem("w_summed"), sem("w_mean_set"), sem("w_quant")
        x_quant, x_backed = sem("x_quant"), sem("x_backed")
        tapped, conved, tanhed, silued = (sem(n) for n in ("tapped", "conved", "tanhed", "silued"))
        h_scaled, h_added, h_quant = sem("h_scaled"), sem("h_added"), [sem(f"h_quant{i}") for i in range(2)]
        v_step, g_step = sem("v_step"), sem("g_step")

        def res_writers(eng, k, t):
            layer, b = BLOCKS[k]
            if t == 0 and layer == 0:
                eng.wait_ge(x_in[min(b, 2)], 16)
            elif t == 1:
                wait_emptied(eng, ("proj_o", k, 0))
            else:
                eng.wait_ge(ffn0_added, b + 1)

        def k_split_aps(t):
            cut = slice(S * t, S * t + S)
            return k_f[:, cut], k_rest[:, cut], [k_parts[:, i, cut] for i in range(3)]

        def q_split_aps():
            return q_f[:, :], q_rest[:, :], [q_parts[:, i, :] for i in range(3)]

        def norm_target(k, t):
            layer, _ = BLOCKS[k]
            return xq[layer] if t == 0 else (z if layer == 0 else xf)

        block = es.enter_context(nc.Block())

        @block.sync
        def _(sp):
            sp.dma_start(proj[:, 0:2, :], projT[:, 0:2, :]).then_inc(proj_in[0], 16)
            sp.dma_start(ctx_sb[:, 0:1, :], ctxT[0:1].rearrange("b d k -> d b k")).then_inc(ctx_in[0], 16)
            sp.wait_ge(minus16_set, 2)

            def place_minus_ones(layer, i):
                for upper in range(2):
                    sp.dma_start(kst[layer][i][64 * upper + 48:64 * upper + 64, :, :], minus16[:, :]).then_inc(k_ones[2 * layer + i], 16)

            def place_zeros(layer, i, done):
                for upper in range(2):
                    sp.dma_start(qst[layer][i][64 * upper + 48:64 * upper + 64, 8 * upper:8 * upper + 8, :], zeros16[:, :]).then_inc(done, 16)

            place_minus_ones(0, 0)
            sp.dma_start(proj[:, 2:8, :], projT[:, 2:8, :]).then_inc(proj_in[1], 16)
            sp.dma_start(mask_i[:, :, :], mask.rearrange("(t p) k -> p t k", p=128)).then_inc(mask_in, 16)
            sp.dma_start(maskT_i[:, :, :], maskT.rearrange("(t p) q -> p t q", p=128)).then_inc(mask_in, 16)
            place_zeros(0, 0, kq_read[0])
            sp.dma_start(w1_sb[:, :], w1T).then_inc(ffn_in, 16)
            sp.dma_start(w2_sb[:, :, :], w2T.rearrange("(c p) n -> p c n", p=128)).then_inc(ffn_in, 16)
            for half in range(FIRST, LAST + 1):
                for task in TASKS.get(half, []):
                    kind, k, t = task
                    if kind == "load_second":
                        sp.dma_start(ctx_sb[:, 1:2, :], ctxT[1:2].rearrange("b d k -> d b k")).then_inc(ctx_in[1], 16)
                        sp.dma_start(res[:, 1, :, :], x[1].rearrange("(t p) d -> p t d", p=128)).then_inc(x_in[1], 16)
                    elif kind == "load_rest":
                        sp.dma_start(rows_sb[:, :, :], rows.partition_broadcast(128)).then_inc(small_in, 16)
                        sp.dma_start(cols_sb[:, :], cols).then_inc(small_in, 16)
                        sp.dma_start(conv_sb[:, :, :], conv.rearrange("(c p) n -> p c n", p=128)).then_inc(small_in, 16)
                        for layer, i in ((0, 1), (1, 0), (1, 1)):
                            place_minus_ones(layer, i)
                            place_zeros(layer, i, kq_read[AT_BLOCK[(layer, i)]])
                        sp.dma_start(ctx_sb[:, 2:B, :], ctxT[2:B].rearrange("b d k -> d b k")).then_inc(ctx_in[2], 16)
                        sp.dma_start(res[:, 2:B, :, :].rearrange("p b t d -> p (b t) d"),
                                     x[2:B].rearrange("b (t p) d -> p (b t) d", p=128)).then_inc(x_in[2], 16)
                    elif kind == "write_k":
                        sp.wait_ge(k_split, NTH[("split_k", k, 1)] + 1)
                        for lo, n in ((0, 3), (3, 2), (5, 1)):
                            sp.dma_start(k_scratch[k, lo:lo + n].rearrange("p r c -> r p c"), k_parts[:, 0:n, :]).then_inc(k_written, 16)
                    elif kind == "write_q":
                        wait_emptied(sp, ("proj_q", k, 0))
                        for part, (lo, n) in enumerate(((0, 3), (3, 2), (5, 1))):
                            if part:
                                sp.wait_ge(q_split, 2 * NTH[("split_q", k, 0)] + part)
                            sp.dma_start(q_scratch[k, lo:lo + n].rearrange("p r c -> r p c"),
                                         q_parts[:, part:part + 1, :].broadcast_to([128, n, S])).then_inc(q_written, 16)
                    elif kind == "read_k":
                        layer, b = BLOCKS[k]
                        old = AT_BLOCK.get((layer, b - 2))
                        if old is not None:
                            sp.wait_ge(st_filled, 2 * PER_BLOCK * (old + 1))
                        sp.wait_ge(k_written, 48 * (NTH[("write_k", k, 0)] + 1))
                        for upper in range(2):
                            sp.dma_start(kst[layer][b % 2][64 * upper:64 * upper + 48, :, :],
                                         k_scratch[k].rearrange("p (d h) c -> (p d) h c", d=DH)[:, 8 * upper:8 * upper + 8, :]).then_inc(kq_read[k], 16)
                    elif kind == "read_q":
                        layer, b = BLOCKS[k]
                        old = AT_BLOCK.get((layer, b - 2))
                        if old is not None:
                            sp.wait_ge(st_filled, 2 * PER_BLOCK * (old + 1))
                            place_zeros(layer, b % 2, kq_read[k])
                        sp.wait_ge(q_written, 48 * (NTH[("write_q", k, 0)] + 1))
                        for upper in range(2):
                            heads = slice(8 * upper, 8 * upper + 8)
                            sp.dma_start(qst[layer][b % 2][64 * upper:64 * upper + 48, heads, :],
                                         q_scratch[k].rearrange("p (d h) c -> (p d) h c", d=DH)[:, heads, :]).then_inc(kq_read[k], 16)
                    elif kind == "max_t":
                        layer, b = BLOCKS[k // NJ]
                        j = k % NJ
                        wait_emptied(sp, task)
                        for part in range(2):
                            row = 64 * (HG * j // 8) + 6 * DH + part
                            sp.dma_start(qst[layer][b % 2][row:row + 1, HG * j:HG * j + HG, :],
                                         max_rows[k % 2][HG * part:HG * part + HG, :]).then_inc(max_placed[k % 2], 16)
                    elif kind == "store":
                        _, b = BLOCKS[k]
                        wait_emptied(sp, ("down", k, 0))
                        sp.dma_start(out[b].rearrange("(t p) d -> p t d", p=128), y_out[:, :, :]).then_inc(stored, 16)
            sp.wait_ge(stored, 16 * B)

        @block.gpsimd
        def _(pool):
            chain = [0]

            def link(ins):
                chain[0] += 1
                ins.then_inc(g_step, 1)
                pool.wait_ge(g_step, chain[0])

            nc.gpsimd.memset(minus16[:, :], -1.0).then_inc(minus16_set, 1)
            nc.gpsimd.memset(zeros16[:, :], 0.0).then_inc(minus16_set, 1)
            nc.gpsimd.memset(id32[:, :], 0.0).then_inc(g_step, 1)
            nc.gpsimd.memset(ones[:, :], 1.0).then_inc(ones_set, 1)
            nc.gpsimd.memset(neghalf[:, :], -0.5).then_inc(ones_set, 1)
            for i in range(2):
                nc.gpsimd.memset(round_bias[:, i:i + 1], (ROUND, -ROUND)[i]).then_inc(round_set, 1)
            pool.wait_ge(g_step, 1)
            chain[0] = 1
            link(nc.gpsimd.affine_select(out=id32[:, :], in_=id32[:, :], compare_op=ALU.not_equal, fill=1.0,
                                         base=0, pattern=[[-1, 128]], channel_multiplier=1))
            nc.gpsimd.tensor_copy(id16[:, :], id32[:, :]).then_inc(id_set, 1)
            pool.wait_ge(id_set, 1)
            pool.wait_ge(ones_set, 2)

            def clear_q(layer, i, upper):
                other = qst[layer][i][64 * (1 - upper):64 * (1 - upper) + 64, 8 * upper:8 * upper + 8, :]
                nc.gpsimd.memset(other.rearrange("p h c -> p (h c)").bitcast(f32), 0.0).then_inc(q_zeros, 1)
                pool.wait_ge(q_zeros, 4 * layer + 2 * i + upper + 1)

            def clear_v(layer, i):
                link(nc.gpsimd.memset(vst[layer][i][:, :, :, :].rearrange("p t h d -> p (t h d)"), 0.0))
                nc.gpsimd.memset(vst[layer][i][:, :, :, DH:DH + 1], 1.0).then_inc(v_set[layer][i], 1)
                pool.wait_ge(v_set[layer][i], 1)

            clear_q(0, 0, 0)
            clear_q(0, 0, 1)

            for half in range(FIRST, LAST + 1):
                for task in TASKS.get(half, []):
                    kind, k, t = task
                    if kind == "split_k" and k > 0:
                        wait_emptied(pool, ("proj_k", k, t))
                        src, rest, parts = k_split_aps(t)
                        link(nc.gpsimd.tensor_tensor(rest, src, parts[0], ALU.subtract))
                        link(nc.gpsimd.tensor_copy(parts[1], rest))
                        nc.gpsimd.tensor_tensor(parts[2], rest, parts[1], ALU.subtract).then_inc(k_split, 1)
                    elif kind == "split_q" and k > 0:
                        wait_emptied(pool, ("proj_q", k, 0))
                        n = 2 * NTH[task]
                        src, rest, parts = q_split_aps()
                        link(nc.gpsimd.tensor_tensor(rest, src, parts[0], ALU.subtract))
                        nc.gpsimd.tensor_copy(parts[1], rest).then_inc(q_split, 1)
                        pool.wait_ge(q_split, n + 1)
                        nc.gpsimd.tensor_tensor(parts[2], rest, parts[1], ALU.subtract).then_inc(q_split, 1)
                    elif kind == "clear":
                        for i in (range(1, 2) if k == 0 else range(2)):
                            clear_v(k, i)
                            clear_q(k, i, 0)
                            clear_q(k, i, 1)
                        if k == 1:
                            nc.gpsimd.memset(hid[:, :, :], 0.0).then_inc(hid_set, 1)
                    elif kind == "split_max":
                        pool.wait_ge(max_taken, 8 * (k + 1))
                        if k >= 2:
                            pool.wait_ge(filled, JOB[("max_t", k - 2, 0)] + 1)
                        link(nc.gpsimd.tensor_copy(max_parts[k % 2][:, :, 0, :], row_max[k % 2][:, :, :]))
                        nc.gpsimd.tensor_tensor(max_parts[k % 2][:, :, 1, :], row_max[k % 2][:, :, :],
                                                max_parts[k % 2][:, :, 0, :], ALU.subtract).then_inc(max_split, 1)
                    elif kind == "stats":
                        pool.wait_ge(stats_done, NTH[task] + 1)
                        link(nc.gpsimd.tensor_scalar(var_eps[NTH[task] % NM][:, :], moments[NTH[task] % NM][:, :, 1], EPS, None, ALU.add))
                        nc.gpsimd.tensor_tensor(rstd[NTH[task] % NM][:, :], var_eps[NTH[task] % NM][:, :], neghalf[:, :], ALU.pow).then_inc(rstd_done, 1)
                    elif kind == "norm" and t == 2:
                        layer, b = BLOCKS[k]
                        pool.wait_ge(norm_done, NTH[task] + 1)
                        gamma = rows_sb[:, GAMMA:GAMMA + 1, :].broadcast_to([128, QT, D])
                        beta = rows_sb[:, BETA:BETA + 1, :].broadcast_to([128, QT, D])
                        link(nc.gpsimd.tensor_tensor(z[:, :, :], z[:, :, :], gamma, ALU.mult))
                        link(nc.gpsimd.tensor_tensor(z[:, :, :], z[:, :, :], beta, ALU.add))
                        nc.gpsimd.tensor_tensor(res[:, b, :, :], res[:, b, :, :], z[:, :, :], ALU.add).then_inc(ffn0_added, 1)
                    elif kind == "add_bo":
                        layer, b = BLOCKS[k]
                        if NTH[task] == 0:
                            pool.wait_ge(small_in, 48)
                        pool.wait_ge(norm_done, NTH[("norm", k, 0)] + 1)
                        bo = rows_sb[:, (BO0, BO1)[layer]:(BO0, BO1)[layer] + 1, :].broadcast_to([128, QT, D])
                        nc.gpsimd.tensor_tensor(res[:, b, :, :], res[:, b, :, :], bo, ALU.add).then_inc(bo_added, 1)

        @block.scalar
        def _(act):
            act.dma_start(res[:, 0, :, :], x[0].rearrange("(t p) d -> p t d", p=128)).then_inc(x_in[0], 16)
            for half in range(FIRST, LAST + 1):
                step, odd = half // 2, half % 2
                if 0 <= step < STEPS:
                    layer, _b = BLOCKS[step // PER_BLOCK]
                    act.wait_ge(st_filled, half + 1)
                    if step >= NP and not odd:
                        act.wait_ge(pv_done, step - NP + 1)
                    nc.scalar.activation(probs[step % NP][:, 2 * odd:2 * odd + 2, :], st[half % NST][:, :, :], ACT.Exp,
                                         scale=SCALES[layer]).then_inc(exp_done, 1)
                if odd and step >= KT and step % KT == 0 and step // KT <= UNITS:
                    u = step // KT - 1
                    act.wait_ge(pv_done, KT * (u + 1))
                    if u >= NJ and u % NJ == 0:
                        act.wait_ge(filled, JOB[("out_t", u // NJ - 1, 1)] + 1)
                    nc.scalar.activation(o_raw[:, u % NJ, :], pv[:, :], ACT.Copy).then_inc(pv_emptied, 1)
                for task in TASKS.get(half, []):
                    kind, k, t = task
                    if task in JOB:
                        bank = JOB[task] % 2
                        side, side16 = sides[bank], sides16[bank]
                    if kind in ("proj_k", "x_t", "proj_q", "proj_v", "heads_t", "xq_t", "spread_scale", "hid_t", "hq_t", "max_t"):
                        act.wait_ge(filled, JOB[task] + 1)
                    if kind == "proj_k":
                        layer, b = BLOCKS[k]
                        if NTH[task] >= 2:
                            act.wait_ge(k_split, 2 * (NTH[task] // 2))
                            act.wait_ge(k_written, 48 * (NTH[task] // 2))
                        elif layer == 1:
                            act.wait_ge(small_in, 48)
                        src, _rest, parts = k_split_aps(t)
                        for dst in (parts[0], src):
                            if layer == 0:
                                ins = nc.scalar.activation(dst, side[:, 0:S], ACT.Copy)
                            else:
                                ins = nc.scalar.activation(dst, side[:, 0:S], ACT.Identity, bias=cols_sb[:, 1:2])
                        ins.then_inc(emptied[bank], 1)
                    elif kind == "proj_q":
                        layer, b = BLOCKS[k]
                        if NTH[task]:
                            act.wait_ge(q_split, 2 * NTH[task])
                            act.wait_ge(q_written, 48 * NTH[task])
                        for dst in (q_parts[:, 0, :], q_f[:, :]):
                            if layer == 0:
                                ins = nc.scalar.activation(dst, side[:, 0:S], ACT.Copy)
                            else:
                                ins = nc.scalar.activation(dst, side[:, 0:S], ACT.Identity, bias=cols_sb[:, 0:1])
                        ins.then_inc(emptied[bank], 1)
                    elif kind == "proj_v":
                        layer, b = BLOCKS[k]
                        old = AT_BLOCK.get((layer, b - 2))
                        if old is not None:
                            act.wait_ge(pv_done, PER_BLOCK * (old + 1))
                        if old is None:
                            act.wait_ge(v_set[layer][b], 1)
                        nc.scalar.activation(vst[layer][b % 2][:, 2 * t:2 * t + 2, :, 0:DH],
                                             side[:, 0:S].rearrange("p (t h d) -> p t h d", t=2, h=H), ACT.Copy).then_inc(emptied[bank], 1)
                    elif kind == "x_t":
                        nc.scalar.activation(x_t[:, :], side[:, 0:S], ACT.Copy).then_inc(emptied[bank], 1)
                    elif kind == "heads_t":
                        nc.scalar.activation(o_t[:, :], side[:, 0:S], ACT.Copy).then_inc(emptied[bank], 1)
                    elif kind == "xq_t":
                        nc.scalar.activation(a_t[:, :], side16[:, 0:S], ACT.Copy).then_inc(emptied[bank], 1)
                    elif kind == "spread_scale":
                        nc.scalar.activation(back_rows[:, :], side[:, 0:S], ACT.Copy).then_inc(emptied[bank], 1)
                    elif kind == "hq_t":
                        nc.scalar.activation(h_t[:, t, :, :].rearrange("p c n -> p (c n)"), side16[:, 0:HID], ACT.Copy).then_inc(emptied[bank], 1)
                    elif kind == "max_t":
                        if k >= 2:
                            act.wait_ge(max_placed[k % 2], 32 * (k // 2))
                        nc.scalar.activation(max_rows[k % 2][:, :], side16[0:2 * HG, 0:S], ACT.Copy).then_inc(emptied[bank], 1)
                    elif kind == "round_h" and t == 1:
                        n = NTH[("scale_h", k, 0)]
                        act.wait_ge(h_scaled, n + 1)
                        if n:
                            act.wait_ge(filled, JOB[[q for q in JOB if q[0] == "hq_t"][QT * n - 1]] + 1)
                        else:
                            act.wait_ge(round_set, 2)
                        nc.scalar.activation(h_tmp[:, t, :], h_tmp[:, t, :], ACT.Identity, bias=round_bias[:, 0:1],
                                             scale=h_scale[:, t:t + 1]).then_inc(h_added, 1)
                        act.wait_ge(h_added, n + 1)
                        nc.scalar.activation(h_q[:, t, :], h_tmp[:, t, :], ACT.Identity, bias=round_bias[:, 1:2]).then_inc(h_quant[1], 1)
                    elif kind == "tap":
                        wait_emptied(act, ("up", k, t))
                        if NTH[task] >= 2:
                            act.wait_ge(filled, JOB[[q for q in JOB if q[0] == "hid_t"][2 * (NTH[task] // 2) - 1]] + 1)
                        if NTH[task] == 0:
                            act.wait_ge(small_in, 48)
                        for c in (2 * t, 2 * t + 1):
                            nc.scalar.activation(y[:, c, :], hid[:, c, 1:S + 1], ACT.Identity, bias=conv_sb[:, c, 3:4],
                                                 scale=conv_sb[:, c, 1:2]).then_inc(tapped, 1)
                    elif kind == "silu":
                        act.wait_ge(conved, 2 * NTH[task] + 2)
                        nc.scalar.activation(tanh_y[:, 2 * t:2 * t + 2, :], y[:, 2 * t:2 * t + 2, :], ACT.Tanh, scale=0.5).then_inc(tanhed, 1)
                    elif kind == "hid_t":
                        if NTH[task] >= QT:
                            act.wait_ge(h_quant[t], NTH[task] // QT)
                        nc.scalar.activation(h_tmp[:, t, :], side[:, :], ACT.Copy).then_inc(emptied[bank], 1)

        @block.vector
        def _(dve):
            chain = [0]

            def link(ins):
                chain[0] += 1
                ins.then_inc(v_step, 1)
                dve.wait_ge(v_step, chain[0])

            link(nc.vector.memset(vst[0][0][:, :, :, :].rearrange("p t h d -> p (t h d)"), 0.0))
            nc.vector.memset(vst[0][0][:, :, :, DH:DH + 1], 1.0).then_inc(v_set[0][0], 1)
            for half in range(FIRST, LAST + 1):
                count = half + LEAD
                u, n = count // 8, count % 8
                if 0 <= u < UNITS:
                    layer, _b = BLOCKS[u // NJ]
                    if u >= 2 and n == 0:
                        dve.wait_ge(max_split, u - 1)
                    if layer == 1 and u // NJ == AT_BLOCK[(1, 0)] and n == 0:
                        dve.wait_ge(mask_set, 1)
                    dve.wait_ge(sm_filled, count + 1)
                    m_out = row_max[u % 2][:, n // HG, n % HG:n % HG + 1]
                    if layer == 0:
                        nc.vector.tensor_reduce(m_out, sm[count % 2][:, :], X, ALU.max).then_inc(max_taken, 1)
                    else:
                        dve.wait_ge(max_taken, count - 1)
                        nc.vector.tensor_tensor_reduce(masked[:, n % 2, :], sm[count % 2][:, :], mask_max[:, n // HG, :],
                                                       1.0, MASK_EXP, ALU.add, ALU.max, m_out).then_inc(max_taken, 1)
                for task in TASKS.get(half, []):
                    kind, k, t = task
                    if task in JOB:
                        bank = JOB[task] % 2
                        side = sides[bank]
                    if kind == "stats":
                        layer, b = BLOCKS[k]
                        src = z if (layer == 0 and t == 2) else res[:, b, :, :]
                        if layer == 0 and t == 2:
                            dve.wait_ge(norm_done, NTH[("norm", k, 1)] + 1)
                        else:
                            res_writers(dve, k, t)
                        m = NTH[task] % NM
                        if NTH[task] >= NM:
                            dve.wait_ge(norm_done, NTH[task] - NM + 1)
                        for i in range(QT):
                            ins = nc.vector.bn_stats(bn[m][:, i, :], src[:, i, :])
                        link(ins)
                        for i in range(QT):
                            ins = nc.vector.bn_aggr(moments[m][:, i, :], bn[m][:, i, :])
                        ins.then_inc(stats_done, 1)
                    elif kind == "norm":
                        layer, b = BLOCKS[k]
                        dst, m = norm_target(k, t), NTH[task] % NM
                        src = z if (layer == 0 and t == 2) else res[:, b, :, :]
                        dve.wait_ge(rstd_done, NTH[task] + 1)
                        if t == 0:
                            before = [q for q in JOB if q[0] == "x_t" and BLOCKS[q[1]][0] == layer and NTH[q] < NTH[("x_t", k, 0)]]
                            if before:
                                dve.wait_ge(filled, JOB[before[-1]] + 1)
                        if layer == 0 and t == 1 and b:
                            dve.wait_ge(ffn0_added, b)
                        for i in range(QT):
                            ins = nc.vector.tensor_scalar(dst[:, i, :], src[:, i, :], moments[m][:, i, 0:1], rstd[m][:, i:i + 1],
                                                          ALU.subtract, ALU.mult)
                        ins.then_inc(norm_done, 1)
                    elif kind == "out_t":
                        dve.wait_ge(filled, JOB[task] + 1)
                        if NTH[task] >= QT and t == 0:
                            dve.wait_ge(filled, JOB[[q for q in JOB if q[0] == "heads_t"][NTH[task] // QT - 1]] + 1)
                        o_nat = side[:, :].rearrange("p (j g c) -> p j g c", j=NJ, g=HG)
                        link(nc.vector.reciprocal(inv_den[:, t, :, :], o_nat[:, :, :, DH]))
                        nc.vector.tensor_tensor(o_heads[:, t, :, :],
                                                side[:, :].rearrange("p (h c) -> p h c", h=H)[:, :, 0:DH],
                                                inv_den[:, t, :, :].rearrange("p j g -> p (j g)").unsqueeze(2).broadcast_to([128, H, DH]),
                                                ALU.mult).then_inc(emptied[bank], 1)
                    elif kind == "proj_o":
                        layer, b = BLOCKS[k]
                        dve.wait_ge(filled, JOB[task] + 1)
                        dve.wait_ge(bo_added, NTH[("add_bo", k, 0)] + 1)
                        flat = res[:, b, :, :].rearrange("p t d -> p (t d)")
                        nc.vector.tensor_tensor(flat, side[:, 0:S], flat, ALU.add).then_inc(emptied[bank], 1)
                    elif kind == "weight_mean":
                        dve.wait_ge(ffn_in, 32)
                        nc.vector.tensor_reduce(w_sum[:, 0:1], w1_sb[:, :], X, ALU.add, apply_absolute_value=True).then_inc(w_summed, 1)
                        nc.vector.tensor_reduce(w_sum[:, 1:2], w2_sb[:, :, :].rearrange("p c n -> p (c n)"), X, ALU.add,
                                                apply_absolute_value=True).then_inc(w_summed, 1)
                        dve.wait_ge(filled, JOB[task] + 1)
                        nc.vector.tensor_scalar(w_mean[:, :], side[:, 0:2], 1.0 / (D * HID), EPS, ALU.mult, ALU.max).then_inc(emptied[bank], 1)
                        wait_emptied(dve, task)
                        nc.vector.reciprocal(w_inv[:, :], w_mean[:, :]).then_inc(w_mean_set, 1)
                    elif kind == "mask":
                        dve.wait_ge(mask_in, 32)
                        nc.vector.tensor_scalar(mask_max[:, :, :], mask_i[:, :, :], 0.0, MASK_MAX, ALU.is_equal, ALU.mult).then_inc(mask_set, 1)
                        for i in range(2):
                            nc.vector.tensor_scalar(mask_exp[:, :, i, :], maskT_i[:, :, :], 0.0, MASK_EXP, ALU.is_equal, ALU.mult).then_inc(mask_set, 1)
                    elif kind == "quant_w":
                        dve.wait_ge(w_mean_set, 1)
                        for i, (w, q) in enumerate(((w1_sb[:, :], w1_q[:, :]),
                                                    (w2_sb[:, :, :].rearrange("p c n -> p (c n)"),
                                                     w2_q[:, :, :].rearrange("p c n -> p (c n)")))):
                            link(nc.vector.tensor_scalar(w_tmp, w, w_inv[:, i:i + 1], ROUND, ALU.mult, ALU.add))
                            link(nc.vector.tensor_scalar(w_tmp, w_tmp, ROUND, 1.0, ALU.subtract, ALU.min))
                            ins = nc.vector.tensor_scalar(q, w_tmp, -1.0, None, ALU.max)
                            if i == 0:
                                link(ins)
                        ins.then_inc(w_quant, 1)
                    elif kind == "split_k" and k == 0:
                        wait_emptied(dve, ("proj_k", k, t))
                        src, rest, parts = k_split_aps(t)
                        link(nc.vector.tensor_tensor(rest, src, parts[0], ALU.subtract))
                        link(nc.vector.tensor_copy(parts[1], rest))
                        nc.vector.tensor_tensor(parts[2], rest, parts[1], ALU.subtract).then_inc(k_split, 1)
                    elif kind == "split_q" and k == 0:
                        wait_emptied(dve, ("proj_q", k, 0))
                        n = 2 * NTH[task]
                        src, rest, parts = q_split_aps()
                        link(nc.vector.tensor_tensor(rest, src, parts[0], ALU.subtract))
                        nc.vector.tensor_copy(parts[1], rest).then_inc(q_split, 1)
                        dve.wait_ge(q_split, n + 1)
                        nc.vector.tensor_tensor(parts[2], rest, parts[1], ALU.subtract).then_inc(q_split, 1)
                    elif kind == "max_x":
                        dve.wait_ge(norm_done, NTH[("norm", k, 1)] + 1)
                        link(nc.vector.tensor_reduce(amax[:, :], xf[:, :, :], X, ALU.max, apply_absolute_value=True))
                        link(nc.vector.tensor_scalar(amax[:, :], amax[:, :], EPS, 1.0 / 127.0, ALU.max, ALU.mult))
                        nc.vector.tensor_scalar(a_back[:, :], amax[:, :], w_mean[:, 0:1], None, ALU.mult)
                        link(nc.vector.reciprocal(a_scale[:, :], amax[:, :]))
                    elif kind == "round_x":
                        if NTH[task]:
                            dve.wait_ge(filled, JOB[[q for q in JOB if q[0] == "xq_t"][NTH[task] - 1]] + 1)
                        for i in range(QT):
                            ins = nc.vector.tensor_scalar(a_tmp[:, i, :], xf[:, i, :], a_scale[:, i:i + 1], ROUND, ALU.mult, ALU.add)
                        link(ins)
                        nc.vector.tensor_scalar(a_q[:, :, :], a_tmp[:, :, :], ROUND, None, ALU.subtract).then_inc(x_quant, 1)
                    elif kind == "back_x":
                        if NTH[task]:
                            dve.wait_ge(filled, JOB[[q for q in JOB if q[0] == "spread_scale"][NTH[task] - 1]] + 1)
                        for i in range(QT):
                            ins = nc.vector.tensor_scalar(back_diag[:, i, :], id32[:, :], a_back[:, i:i + 1], None, ALU.mult)
                        ins.then_inc(x_backed, 1)
                    elif kind == "up":
                        dve.wait_ge(filled, JOB[task] + 1)
                        if t == 0:
                            wait_emptied(dve, ("spread_scale", k, 0))
                            if NTH[task] == 0:
                                dve.wait_ge(hid_set, 1)
                            else:
                                dve.wait_ge(tapped, CH * (NTH[task] // 2))
                        nc.vector.tensor_tensor(hid[:, 2 * t:2 * t + 2, 1:S + 1],
                                                side[:, :].rearrange("p (c s) -> p c s", c=2),
                                                back_rows[:, :].unsqueeze(1).broadcast_to([128, 2, S]), ALU.mult).then_inc(emptied[bank], 1)
                    elif kind == "conv":
                        dve.wait_ge(tapped, NTH[task] + 1)
                        link(nc.vector.scalar_tensor_tensor(y[:, t, :], hid[:, t, 0:S], conv_sb[:, t, 0:1], y[:, t, :],
                                                            ALU.mult, ALU.add))
                        nc.vector.scalar_tensor_tensor(y[:, t, :], hid[:, t, 2:S + 2], conv_sb[:, t, 2:3], y[:, t, :],
                                                       ALU.mult, ALU.add).then_inc(conved, 1)
                    elif kind == "silu":
                        dve.wait_ge(tanhed, NTH[task] + 1)
                        flat = [a[:, 2 * t:2 * t + 2, :].rearrange("p c s -> p (c s)") for a in (tanh_y, y)]
                        nc.vector.scalar_tensor_tensor(flat[1], flat[0], 1.0, flat[1], ALU.add, ALU.mult).then_inc(silued, 1)
                    elif kind == "max_h":
                        wait_emptied(dve, ("hid_t", k, t))
                        ins = nc.vector.tensor_reduce(h_max[:, t:t + 1], h_tmp[:, t, :], X, ALU.max, apply_absolute_value=True)
                        if t == 1:
                            link(ins)
                    elif kind == "scale_h":
                        link(nc.vector.tensor_scalar(h_max[:, :], h_max[:, :], 2 * EPS, 1.0 / 127.0, ALU.max, ALU.mult))
                        nc.vector.tensor_scalar(h_back[:, :], h_max[:, :], w_mean[:, 1:2], 0.5, ALU.mult, ALU.mult)
                        nc.vector.reciprocal(h_scale[:, :], h_max[:, :]).then_inc(h_scaled, 1)
                        dve.wait_ge(h_scaled, NTH[task] + 1)
                    elif kind == "round_h" and t == 0:
                        if NTH[task] >= QT:
                            dve.wait_ge(filled, JOB[[q for q in JOB if q[0] == "hq_t"][NTH[task] - QT]] + 1)
                        link(nc.vector.tensor_scalar(h_tmp[:, t, :], h_tmp[:, t, :], h_scale[:, t:t + 1], ROUND, ALU.mult, ALU.add))
                        nc.vector.tensor_scalar(h_q[:, t, :], h_tmp[:, t, :], ROUND, None, ALU.subtract).then_inc(h_quant[0], 1)
                    elif kind == "down":
                        _, b = BLOCKS[k]
                        dve.wait_ge(filled, JOB[task] + 1)
                        if NTH[task]:
                            dve.wait_ge(stored, 16 * NTH[task])
                        for i in range(QT):
                            ins = nc.vector.scalar_tensor_tensor(y_out[:, i, :], side[:, 128 * i:128 * i + 128], h_back[:, i:i + 1],
                                                                 res[:, b, i, :], ALU.mult, ALU.add)
                        ins.then_inc(emptied[bank], 1)

        @block.tensor
        def _(pe):
            def scores_t(n):
                step, odd = n // 2, n % 2
                k, j, kt = step // PER_BLOCK, step // KT % NJ, step % KT
                layer, b = BLOCKS[k]
                ks, qs, u = kst[layer][b % 2], qst[layer][b % 2], step // KT
                if kt == 0 and not odd:
                    pe.wait_ge(max_placed[u % 2], 32 * (u // 2 + 1))
                if n >= NST:
                    pe.wait_ge(exp_done, n - NST + 1)
                if layer == 1:
                    if n == 2 * PER_BLOCK * AT_BLOCK[(1, 0)]:
                        pe.wait_ge(mask_set, 3)
                    nc.tensor.matmul(st[n % NST][:, :, :], id16[:, :], mask_exp[:, kt, :, :], start=True, stop=False)
                for g in range(2):
                    h = HG * j + 2 * odd + g
                    ins = nc.tensor.matmul(st[n % NST][:, g, :], ks[:, h % 8, 128 * kt:128 * kt + 128], qs[:, h, :],
                                           start=layer == 0, stop=layer == 0 or g == 1)
                ins.then_inc(st_filled, 1)

            def scores(u, n):
                k, j, t, g = u // NJ, u % NJ, n // HG, n % HG
                layer, b = BLOCKS[k]
                count = 8 * u + n
                if j == 0 and n == 0:
                    pe.wait_ge(kq_read[k], 96)
                    if b < 2:
                        pe.wait_ge(k_ones[2 * layer + b], 32)
                        pe.wait_ge(q_zeros, 4 * layer + 2 * b + 2)
                if count >= 2:
                    pe.wait_ge(max_taken, count - 1)
                h = HG * j + g
                nc.tensor.matmul(sm[count % 2][:, :], qst[layer][b % 2][:, h, 128 * t:128 * t + 128],
                                 kst[layer][b % 2][:, h % 8, :], start=True, stop=True).then_inc(sm_filled, 1)

            def weighted(step):
                k, j, kt = step // PER_BLOCK, step // KT % NJ, step % KT
                layer, b = BLOCKS[k]
                if step % PER_BLOCK == 0:
                    wait_emptied(pe, ("proj_v", k, 0))
                    wait_emptied(pe, ("proj_v", k, 1))
                u = step // KT
                if kt == 0 and u:
                    pe.wait_ge(pv_emptied, u)
                pe.wait_ge(exp_done, 2 * step + 2)
                for g in range(HG):
                    ins = nc.tensor.matmul(pv[32 * g:32 * g + 32, :], vst[layer][b % 2][:, kt, HG * j + g, :],
                                           probs[step % NP][:, g, :], start=kt == 0, stop=kt == KT - 1)
                ins.then_inc(pv_done, 1)

            def job(task):
                kind, k, t = task
                n = JOB[task]
                side, side16 = sides[n % 2], sides16[n % 2]
                if n >= 2:
                    pe.wait_ge(emptied[n % 2], n // 2)
                if kind == "proj_k":
                    layer, b = BLOCKS[k]
                    if k == 0 and t == 0:
                        pe.wait_ge(proj_in[0], 16)
                    elif layer == 1 and b == 0 and t == 0:
                        pe.wait_ge(proj_in[1], 16)
                    pe.wait_ge(ctx_in[min(b, 2)], 16)
                    ins = nc.tensor.matmul(side[:, 0:S], proj[:, 4 * layer + 1, :], ctx_sb[:, b, S * t:S * t + S], start=True, stop=True)
                elif kind == "proj_v":
                    layer, b = BLOCKS[k]
                    if k == 0 and t == 0:
                        pe.wait_ge(proj_in[1], 16)
                    if layer == 1 and b == 0 and t == 0:
                        pe.wait_ge(small_in, 48)
                    if layer == 1:
                        nc.tensor.matmul(side[:, 0:S].rearrange("p (i d) -> p i d", i=2), ones[0:1, :],
                                         rows_sb[0:1, BV1:BV1 + 1, :].broadcast_to([1, 2, D]), start=True, stop=False)
                    for i in range(2):
                        kt = 2 * t + i
                        ins = nc.tensor.matmul(side[:, 128 * i:128 * i + 128], ctx_sb[:, b, 128 * kt:128 * kt + 128],
                                               proj[:, 4 * layer + 2, :], start=layer == 0, stop=layer == 0 or i == 1)
                elif kind == "x_t":
                    layer, b = BLOCKS[k]
                    pe.wait_ge(norm_done, NTH[("norm", k, 0)] + 1)
                    if NTH[task] == 0:
                        pe.wait_ge(id_set, 1)
                    for i in range(QT):
                        ins = nc.tensor.transpose(side[:, 128 * i:128 * i + 128], xq[layer][:, i, :], id32[:, :])
                elif kind == "proj_q":
                    layer, b = BLOCKS[k]
                    wait_emptied(pe, ("x_t", k, 0))
                    ins = nc.tensor.matmul(side[:, 0:S], proj[:, 4 * layer, :], x_t[:, :], start=True, stop=True)
                elif kind == "max_t":
                    pe.wait_ge(max_split, k + 1)
                    for i in range(QT):
                        ins = nc.tensor.transpose(side16[0:2 * HG, 128 * i:128 * i + 128],
                                                  max_parts[k % 2][:, i, :, :].rearrange("p a g -> p (a g)"), id16[:, :])
                elif kind == "out_t":
                    pe.wait_ge(pv_emptied, NJ * (k + 1))
                    for j in range(NJ):
                        ins = nc.tensor.transpose(side[:, 128 * j:128 * j + 128], o_raw[:, j, 128 * t:128 * t + 128], id32[:, :])
                elif kind == "heads_t":
                    wait_emptied(pe, ("out_t", k, 1))
                    for i in range(QT):
                        ins = nc.tensor.transpose(side[:, 128 * i:128 * i + 128],
                                                  o_heads[:, i, :, :].rearrange("p h d -> p (h d)"), id32[:, :])
                elif kind == "proj_o":
                    layer, b = BLOCKS[k]
                    wait_emptied(pe, ("heads_t", k, 0))
                    for i in range(QT):
                        ins = nc.tensor.matmul(side[:, 128 * i:128 * i + 128], o_t[:, 128 * i:128 * i + 128],
                                               proj[:, 4 * layer + 3, :], start=True, stop=True)
                elif kind == "weight_mean":
                    pe.wait_ge(w_summed, 2)
                    pe.wait_ge(ones_set, 1)
                    ins = nc.tensor.matmul(side[:, 0:2], ones[:, :], w_sum[:, :], start=True, stop=True)
                elif kind == "xq_t":
                    pe.wait_ge(x_quant, NTH[task] + 1)
                    for i in range(QT):
                        ins = nc.tensor.transpose(side16[:, 128 * i:128 * i + 128], a_q[:, i, :], id16[:, :])
                elif kind == "spread_scale":
                    pe.wait_ge(x_backed, NTH[task] + 1)
                    ins = nc.tensor.matmul(side[:, 0:S], ones[:, :], back_diag[:, :, :].rearrange("p t s -> p (t s)"),
                                           start=True, stop=True)
                elif kind == "up":
                    if t == 0:
                        wait_emptied(pe, ("xq_t", k, 0))
                        if NTH[task] == 0:
                            pe.wait_ge(w_quant, 1)
                    for i in range(2):
                        c = 2 * t + i
                        ins = nc.tensor.matmul(side[:, S * i:S * i + S], w1_q[:, 128 * c:128 * c + 128], a_t[:, :],
                                               start=True, stop=True)
                elif kind == "hid_t":
                    pe.wait_ge(silued, NTH[("silu", k, 1)] + 1)
                    for c in range(CH):
                        ins = nc.tensor.transpose(side[:, 128 * c:128 * c + 128], y[:, c, 128 * t:128 * t + 128], id32[:, :])
                elif kind == "hq_t":
                    pe.wait_ge(h_quant[t], NTH[("scale_h", k, 0)] + 1)
                    for c in range(CH):
                        ins = nc.tensor.transpose(side16[:, 128 * c:128 * c + 128], h_q[:, t, 128 * c:128 * c + 128], id16[:, :])
                elif kind == "down":
                    wait_emptied(pe, ("hq_t", k, 1))
                    for i in range(QT):
                        for c in range(CH):
                            ins = nc.tensor.matmul(side[:, 128 * i:128 * i + 128], h_t[:, i, c, :], w2_q[:, c, :],
                                                   start=c == 0, stop=c == CH - 1)
                ins.then_inc(filled, 1)

            for half in range(FIRST, LAST + 1):
                if 0 <= half + 2 < 2 * STEPS:
                    scores_t(half + 2)
                count = half + LEAD
                if 0 <= count < 8 * UNITS:
                    scores(count // 8, count % 8)
                for task in TASKS.get(half, []):
                    if task in JOB:
                        job(task)
                if half % 2 == 0 and 0 <= half // 2 - 1 < STEPS:
                    weighted(half // 2 - 1)


def kernel(**inputs):
    import numpy as np
    import concourse.bacc as bacc
    from concourse.bass_utils import run_bass_kernel_spmd

    a = {name: np.asarray(value) for name, value in inputs.items()}
    by_dim = np.arange(D).reshape(H, DH).T.reshape(-1)
    arrays = {
        "x": a["x"],
        "ctxT": a["ctx_1024"].transpose(0, 2, 1),
        "projT": np.stack([
            a["L0_xattn_Wq"][by_dim].T, a["L0_xattn_Wk"][by_dim].T, a["L0_xattn_Wv"].T, a["L0_xattn_Wo"].T,
            a["L1_xattn_w_q"][by_dim].T, a["L1_xattn_w_k"][by_dim].T, a["L1_xattn_w_v"].T, a["L1_xattn_w_o"].T], axis=1),
        "rows": np.stack([a["L0_xattn_bo"], a["L0_ffn_ln_g"], a["L0_ffn_ln_b"], a["L1_xattn_b_o"], a["L1_xattn_b_v"]]),
        "cols": np.stack([a["L1_xattn_b_q"][by_dim], a["L1_xattn_b_k"][by_dim]], axis=1),
        "mask": a["mask_1x1xSxS2_ik0"][0, 0],
        "maskT": a["mask_1x1xSxS2_ik0"][0, 0].T,
        "w1T": a["L1_ffn_w1"].T,
        "conv": np.concatenate([a["L1_ffn_conv_w"][:, 0, :], a["L1_ffn_conv_b"][:, None]], axis=1),
        "w2T": a["L1_ffn_w2"].T,
    }
    arrays = {name: np.ascontiguousarray(value) for name, value in arrays.items()}
    nc = bacc.Bacc("TRN2", target_bir_lowering=False, num_devices=1)
    aps = [nc.dram_tensor(name, value.shape, mybir.dt.from_np(value.dtype), kind="ExternalInput").ap()
           for name, value in arrays.items()]
    out = nc.dram_tensor("out", (B, S, D), mybir.dt.float32, kind="ExternalOutput").ap()
    build(nc, *aps, out)
    result = run_bass_kernel_spmd(nc, [arrays], core_ids=[0])
    return result.results[0]["out"]
```
